# Optimizing a Trainium2 kernel written in Bass

```python
import numpy as np
import jax
import jax.numpy as jnp

def _softmax(x, axis=-1):
    return jax.nn.softmax(x, axis=axis)

def _gelu(x):
    return jax.nn.gelu(x, approximate=True)

def _silu(x):
    return jax.nn.silu(x)

def _sigmoid(x):
    return jax.nn.sigmoid(x)

def _layernorm(x, axis=-1, eps=1e-05):
    m = jnp.mean(x, axis=axis, keepdims=True)
    v = jnp.var(x, axis=axis, keepdims=True)
    return (x - m) / jnp.sqrt(v + eps)

def _scatter_add(tgt, idx, src, axis=0):
    return tgt.at[idx].add(src)

def _segment_sum(src, seg, n):
    return jax.ops.segment_sum(src, seg, n)
kernel_name = 'mk_flamingo_gated_d1_seqx_r2_de5d1d'

def setup_inputs(seed: int=0):
    np.random.seed(seed)
    _w = jnp.asarray

    def _rec_inputs():
        import jax
        import jax.numpy as jnp
        _rk = jax.random.key(seed)
        x = -0.0002928 + 1 * jax.random.normal(jax.random.fold_in(_rk, 1), (32, 256, 512), jnp.float32)
        _lenS = 256 - jax.random.randint(jax.random.fold_in(_rk, 7), (32,), 0, max(1, 256 // 4) + 1, jnp.int32)
        _lenS2 = 256 - jax.random.randint(jax.random.fold_in(_rk, 8), (32,), 0, max(1, 256 // 4) + 1, jnp.int32)
        _ctx_1024P = jax.random.normal(jax.random.fold_in(_rk, 11), (32, 16, 512), jnp.float32)
        _ctx_1024c = jax.random.dirichlet(jax.random.fold_in(_rk, 511), 0.3 * jnp.ones((16,), jnp.float32), (32, 256))
        _ctx_1024t = jnp.einsum('bsk,bkd->bsd', _ctx_1024c, _ctx_1024P)
        _ctx_1024t = _ctx_1024t * jax.lax.rsqrt(jnp.mean(jnp.square(_ctx_1024t)) + 1e-12) * 0.953939
        ctx_1024 = -1.39393e-06 + 0.999914 * (_ctx_1024t + 0.3 * jax.random.normal(jax.random.fold_in(_rk, 611), (32, 256, 512), jnp.float32))
        _g = jax.random.normal(jax.random.fold_in(_rk, 9001), (2, 1), jnp.float32)
        _g = jnp.sign(_g) * jnp.maximum(jnp.abs(_g), 1.0) + (_g == 0) * 1.0
        g_xattn = _g[0]
        g_ffn = _g[1]
        return (x, ctx_1024, g_xattn, g_ffn)
    x, ctx_1024, g_xattn, g_ffn = _rec_inputs()

    def _L0_xattn_setup():
        import jax, jax.numpy as jnp
        import numpy as np
        D_MODEL = 512
        N_HEADS = 16
        D_K = D_MODEL // N_HEADS
        key = jax.random.key(seed)
        ks = jax.random.split(key, 11)
        B, T = (2, 1024)
        s = 1.0 / np.sqrt(D_MODEL)
        return {'q': jax.random.normal(ks[0], (B, T, D_MODEL), jnp.float32), 'k': jax.random.normal(ks[1], (B, T, D_MODEL), jnp.float32), 'v': jax.random.normal(ks[2], (B, T, D_MODEL), jnp.float32), 'Wq': jax.random.normal(ks[3], (D_MODEL, D_MODEL), jnp.float32) * s, 'bq': jnp.zeros((D_MODEL,), jnp.float32), 'Wk': jax.random.normal(ks[4], (D_MODEL, D_MODEL), jnp.float32) * s, 'bk': jnp.zeros((D_MODEL,), jnp.float32), 'Wv': jax.random.normal(ks[5], (D_MODEL, D_MODEL), jnp.float32) * s, 'bv': jnp.zeros((D_MODEL,), jnp.float32), 'Wo': jax.random.normal(ks[6], (D_MODEL, D_MODEL), jnp.float32) * s, 'bo': jnp.zeros((D_MODEL,), jnp.float32)}
    _L0_xattn_all = _L0_xattn_setup()
    _L0_xattn_in = {k: v for k, v in _L0_xattn_all.items() if k in ('Wq', 'bq', 'Wk', 'bk', 'Wv', 'bv', 'Wo', 'bo')}
    del _L0_xattn_all

    def _L0_ffn_setup():
        import jax, jax.numpy as jnp
        import numpy as np
        B, S, D, E, H, K = (64, 1024, 512, 32, 2048, 8)
        key = jax.random.key(seed)
        k0, k1, k2, k3 = jax.random.split(key, 4)
        x = jax.random.normal(k0, (B, S, D), jnp.float32)
        gate_w = jax.random.normal(k1, (E, D), jnp.float32) * (1.0 / np.sqrt(D))
        gate_b = jnp.zeros((E,), jnp.float32)
        w1 = jax.random.normal(k2, (E, D + 1, H), jnp.float32) * (1.0 / np.sqrt(D + 1))
        w2 = jax.random.normal(k3, (E, H + 1, D), jnp.float32) * (1.0 / np.sqrt(H + 1))
        return {'x': x, 'gate_w': gate_w, 'gate_b': gate_b, 'w1': w1, 'w2': w2}
    _L0_ffn_all = _L0_ffn_setup()
    _L0_ffn_in = {k: v for k, v in _L0_ffn_all.items() if k in ('gate_w', 'gate_b', 'w1', 'w2')}
    del _L0_ffn_all
    return {'x': x, 'ctx_1024': ctx_1024, 'g_xattn': g_xattn, 'g_ffn': g_ffn, 'L0_xattn_Wq': _L0_xattn_in['Wq'], 'L0_xattn_bq': _L0_xattn_in['bq'], 'L0_xattn_Wk': _L0_xattn_in['Wk'], 'L0_xattn_bk': _L0_xattn_in['bk'], 'L0_xattn_Wv': _L0_xattn_in['Wv'], 'L0_xattn_bv': _L0_xattn_in['bv'], 'L0_xattn_Wo': _L0_xattn_in['Wo'], 'L0_xattn_bo': _L0_xattn_in['bo'], 'L0_ffn_gate_w': _L0_ffn_in['gate_w'], 'L0_ffn_gate_b': _L0_ffn_in['gate_b'], 'L0_ffn_w1': _L0_ffn_in['w1'], 'L0_ffn_w2': _L0_ffn_in['w2']}

def reference(x, ctx_1024, g_xattn, g_ffn, L0_xattn_Wq, L0_xattn_bq, L0_xattn_Wk, L0_xattn_bk, L0_xattn_Wv, L0_xattn_bv, L0_xattn_Wo, L0_xattn_bo, L0_ffn_gate_w, L0_ffn_gate_b, L0_ffn_w1, L0_ffn_w2):
    import jax
    import jax.numpy as jnp

    def _L0_xattn_ref(q, k, v, Wq, bq, Wk, bk, Wv, bv, Wo, bo):
        import jax, jax.numpy as jnp
        import numpy as np
        D_MODEL = 512
        N_HEADS = 16
        D_K = D_MODEL // N_HEADS
        B, T, _ = q.shape
        H, dk = (N_HEADS, D_K)

        def split_heads(x):
            return x.reshape(B, T, H, dk).transpose(0, 2, 1, 3)
        qh = split_heads(q @ Wq + bq)
        kh = split_heads(k @ Wk + bk)
        vh = split_heads(v @ Wv + bv)
        scores = jnp.einsum('bhqd,bhkd->bhqk', qh, kh) / jnp.sqrt(jnp.float32(dk))
        attn = jax.nn.softmax(scores, axis=-1)
        ctx = jnp.einsum('bhqk,bhkd->bhqd', attn, vh)
        ctx = ctx.transpose(0, 2, 1, 3).reshape(B, T, D_MODEL)
        return ctx @ Wo + bo

    def _L0_ffn_ref(x, gate_w, gate_b, w1, w2):
        import jax, jax.numpy as jnp
        import numpy as np
        B, S, D, E, H, K = (64, 1024, 512, 32, 2048, 8)
        b, s, d = x.shape
        logits = jnp.einsum('bsd,ed->bse', x, gate_w) + gate_b
        probs = jax.nn.softmax(logits, axis=-2)
        vals_t, idx_t = jax.lax.top_k(probs.transpose(0, 2, 1), K)
        vals = vals_t.transpose(0, 2, 1)
        idx = idx_t.transpose(0, 2, 1)
        flat_idx = idx.reshape(b, K * E)
        tok = jnp.take_along_axis(x, flat_idx[:, :, None], axis=1)
        tok = tok.reshape(b, K, E, d)
        merged = jnp.einsum('bked,bke->bed', tok, vals)
        ones = jnp.ones(merged.shape[:-1] + (1,), merged.dtype)
        h = jnp.einsum('bei,eih->beh', jnp.concatenate([merged, ones], -1), w1)
        h = jax.nn.gelu(h, approximate=False)
        o = jnp.einsum('bej,ejo->beo', jnp.concatenate([h, ones], -1), w2)
        out_tok = jnp.einsum('beo,bke->bkeo', o, vals).reshape(b, K * E, d)
        out = jnp.zeros_like(x).at[jnp.arange(b)[:, None], flat_idx].add(out_tok)
        return out
    x = x + jnp.tanh(g_xattn[0]) * _L0_xattn_ref(_layernorm(x, axis=-1), ctx_1024, ctx_1024, L0_xattn_Wq, L0_xattn_bq, L0_xattn_Wk, L0_xattn_bk, L0_xattn_Wv, L0_xattn_bv, L0_xattn_Wo, L0_xattn_bo)
    x = x + jnp.tanh(g_ffn[0]) * _L0_ffn_ref(_layernorm(x, axis=-1), L0_ffn_gate_w, L0_ffn_gate_b, L0_ffn_w1, L0_ffn_w2)
    return x

_drawn_inputs = setup_inputs


def setup_inputs(seed=0):
    import zlib

    import numpy as np

    out = dict(_drawn_inputs(seed))
    spreads = {'L0_xattn_bq': (0.0, 0.522),
     'L0_xattn_bk': (0.0, 0.8),
     'L0_xattn_bv': (0.0, 0.1),
     'L0_xattn_bo': (0.0, 0.1),
     'L0_ffn_gate_b': (0.0, 0.8)}
    factors = {}
    for name, (base, spread) in spreads.items():
        noise = np.random.default_rng([zlib.crc32(name.encode()), seed]).standard_normal(out[name].shape)
        drawn = base * np.exp(spread * noise) if base else spread * noise
        out[name] = jnp.asarray(drawn.astype(out[name].dtype))
    for name, factor in factors.items():
        out[name] = (out[name] * factor).astype(out[name].dtype)
    return out
```

```python
from contextlib import ExitStack

import numpy as np

import concourse.bass as bass
from concourse import mybir
from concourse.alu_op_type import AluOpType as ALU

F32 = mybir.dt.float32
F32R = mybir.dt.float32r
ACT = mybir.ActivationFunctionType
AX = mybir.AxisListType

B, T, D = 32, 256, 512
H, DK = 16, 32
E, HID, TOP = 32, 2048, 8
P = 128
KC = D // P
TT = T // P
GB = 4
NG = B // GB
HB = H // 4
SCALE = float(DK) ** -0.5
EPS = 1e-5


def after(eng, sem, count):
    if isinstance(count, int) and count <= 0:
        return
    eng.wait_ge(sem, count)


def after_apart(eng, sem, count, passed):
    if isinstance(count, int) and count <= 0:
        return
    eng.wait_ge(sem, count)
    eng.sem_inc(passed, 1)


def run_batches(eng, step):
    for b in range(-2, 2 * GB):
        step(b, b // GB, b % GB)
    with eng.Fori(2, NG - 1) as g:
        for k in range(GB):
            step(g * GB + k, g, k)
    for b in range(B - GB, B + 2):
        step(b, b // GB, b % GB)


def has(b, low, high):
    return low <= b < high if isinstance(b, int) else True


def attention_and_routing(nc, x, ctx, g_xattn, wq, bq, wk, bk, wv, bv, wo, bo, gate_w, gate_b, out, merged_dram,
                          picked_dram):
    st = ExitStack()
    with st:
        sb = lambda name, shape, dt=F32: st.enter_context(nc.sbuf_tensor(name, shape, dt))
        ps = lambda name: st.enter_context(nc.psum_tensor(name, [P, 512], F32))
        sem = lambda name: st.enter_context(nc.semaphore(name))

        w_q, w_k, w_v, w_o = (sb(n, [P, 2, KC, D], F32R) for n in ("w_q", "w_k", "w_v", "w_o"))
        q_stack = sb("q_stack", [P, H, T], F32R)
        k_stack = sb("k_stack", [P, H, T], F32R)
        xt = sb("xt", [P, TT, D])
        ct = sb("ct", [P, TT, D])
        xT = sb("xT", [P, 2, KC, T], F32R)
        cT = sb("cT", [P, 2, KC, T], F32R)
        qk = sb("qk", [P, 4, HB, T])
        v = sb("v", [P, 2, TT, D])
        pr = sb("pr", [P, 2, TT, T])
        pT = sb("pT", [P, 4, TT, T])
        den = sb("den", [P, 2, H // 2, TT])
        rden = sb("rden", [P, TT, H // 2, DK])
        negmax = sb("negmax", [P, 2, TT])
        o_n = sb("o_n", [P, 2, 2, T])
        oT = sb("oT", [P, 2, KC, T], F32R)
        x2 = sb("x2", [P, GB, TT, D])
        x2T = sb("x2T", [P, KC, T])
        lg = sb("lg", [P, T])
        rest = sb("rest", [P, T])
        picked = sb("picked", [P, T])
        pickedT = sb("pickedT", [P, TT, P])
        merged = sb("merged", [P, D])
        mergedT = sb("mergedT", [P, KC, P])
        top8 = sb("top8", [P, TOP])
        rt = sb("rt", [P, 4])
        ln1 = sb("ln1", [P, 32])
        ln2 = sb("ln2", [P, 32])
        ident = sb("ident", [P, P])
        ones = sb("ones", [1, P])
        bv_col = sb("bv_col", [P, KC])
        res_bias = sb("res_bias", [P, D])
        bqk = sb("bqk", [P, 3, HB])
        gwT = sb("gwT", [P, KC, E])
        gb = sb("gb", [P, 1])
        gate = sb("gate", [P, 2])
        eps = sb("eps", [P, 1])

        S = [ps("S0"), ps("S1")]
        TP = [ps("TP0"), ps("TP1")]
        A = [ps("A0"), ps("A1")]
        O = ps("O")
        M = ps("M")

        load = [sem(f"load_{n}") for n in ("wq", "wk", "wv", "wo")]
        small, const, split_hi, split_lo, setup_mm, setup_v, setup_a = (
            sem(n) for n in ("small", "const", "split_hi", "split_lo", "setup_mm", "setup_v", "setup_a"))
        bv_wide = ct[:, 0, :].rearrange("p (k m) -> p k m", k=KC)
        bo_row, gw = ct[0:1, 1, :], xt[0:E, 0, :]
        raw = [qk[:, 2 * i:2 * i + 2, :, :].rearrange("p a c t -> p (a c t)").rearrange("p (k n) -> p k n", k=KC)
               for i in range(2)]
        raw += [x2[:, 2 * i:2 * i + 2, :, :].rearrange("p a c t -> p (a c t)").rearrange("p (k n) -> p k n", k=KC)
                for i in range(2)]
        weights = [w_q, w_k, w_v, w_o]

        def pieces(i, k):
            if i >= 2:
                return [(raw[i][:, k, :], [weights[i][:, half, k, :] for half in range(2)])]
            src = raw[i][:, k, :].rearrange("p (j c d) -> p c j d", j=4, c=4)
            return [(src[:, c], [weights[i][:, half, k, P * c:P * c + P].rearrange("p (j d) -> p j d", j=4)
                                 for half in range(2)]) for c in range(4)]

        n_small = 8 + 2 + 4 + 2
        with nc.Block() as block:

            @block.sync
            def _(sp):
                for i, w in enumerate((wq, wk, wv, wo)):
                    sp.dma_start(raw[i], w.rearrange("(k p) n -> p k n", p=P)).then_inc(load[i], 16)

            @block.gpsimd
            def _(pool):
                for i, bias in enumerate((bq, bk)):
                    for j in range(4):
                        pool.dma_start(bqk[32 * j:32 * j + 32, i, :],
                                       bias[P * j:P * j + P].rearrange("(c d) -> d c", d=DK),
                                       allow_slow_non_contiguous=True).then_inc(small, 16)
                pool.dma_start(bv_col[:], bv.rearrange("(k p) -> p k", p=P),
                               allow_slow_non_contiguous=True).then_inc(small, 16)
                pool.dma_start(bo_row, bo.rearrange("(a n) -> a n", a=1)).then_inc(small, 16)
                for j in range(GB):
                    pool.dma_start(gb[E * j:E * j + E, :], gate_b.rearrange("(e a) -> e a", a=1)).then_inc(small, 16)
                pool.dma_start(gw, gate_w).then_inc(small, 16)
                pool.dma_start(gate[:, 0:1], g_xattn.rearrange("(a n) -> a n", a=1).broadcast_to([P, 1])).then_inc(small, 16)
                pool.memset(ident[:], 0.0).then_inc(const, 1)
                pool.wait_ge(const, 1)
                pool.affine_select(out=ident[:], in_=ident[:], compare_op=ALU.not_equal, fill=1.0, base=0,
                                   pattern=[[-1, P]], channel_multiplier=1).then_inc(const, 1)
                pool.memset(ones[:], 1.0).then_inc(const, 1)
                pool.memset(eps[:], EPS).then_inc(const, 1)

            @block.scalar
            def _(act):
                for i in range(4):
                    act.wait_ge(load[i], 16)
                    for k in range(KC):
                        for src, dst in pieces(i, k):
                            last = act.activation(dst[0], src, ACT.Copy, scale=SCALE if i == 0 else 1.0)
                        last.then_inc(split_hi, 1)
                act.wait_ge(small, 16 * n_small)
                act.activation(gate[:, 1:2], gate[:, 0:1], ACT.Tanh).then_inc(setup_a, 1)
                act.wait_ge(setup_a, 1)
                act.wait_ge(setup_mm, 1)
                act.activation(res_bias[:], A[0][:, :], ACT.Copy, scale=gate[:, 1:2]).then_inc(setup_a, 1)
                act.wait_ge(setup_mm, 2)
                act.activation(gwT[:].rearrange("p k e -> p (k e)"), A[1][:, 0:KC * E], ACT.Copy).then_inc(setup_a, 1)

            @block.vector
            def _(dve):
                dve.wait_ge(small, 16 * n_small)
                dve.tensor_scalar(bqk[:, 2, :], bqk[:, 0, :], SCALE, None, ALU.mult).then_inc(setup_v, 1)
                for k in range(KC):
                    dve.tensor_copy(bv_wide[:, k, :], bv_col[:, k:k + 1].broadcast_to([P, P])).then_inc(setup_v, 1)
                for i in range(4):
                    dve.wait_ge(load[i], 16)
                    for k in range(KC):
                        dve.wait_ge(split_hi, KC * i + k + 1)
                        for src, dst in pieces(i, k):
                            last = dve.scalar_tensor_tensor(dst[1], src, SCALE if i == 0 else 1.0, dst[0], ALU.mult,
                                                            ALU.subtract)
                        last.then_inc(split_lo, 1)

            @block.tensor
            def _(pe):
                pe.wait_ge(setup_v, 1 + KC)
                pe.wait_ge(const, 4)
                pe.wait_ge(load[3], 16)
                pe.wait_ge(small, 16 * n_small)
                for k in range(KC):
                    nc.tensor.matmul(A[0][:, :], bv_wide[:, k, :], raw[3][:, k, :], start=(k == 0), stop=False)
                nc.tensor.matmul(A[0][:, :], ones[:], bo_row, start=False, stop=True).then_inc(setup_mm, 1)
                for k in range(KC):
                    last = nc.tensor.transpose(A[1][:, E * k:E * k + E], gw[:, P * k:P * k + P], ident[0:E, 0:E])
                last.then_inc(setup_mm, 1)

        x_in, c_in, x2_out, m_out, p_out = (sem(n) for n in ("x_in", "c_in", "x2_out", "m_out", "p_out"))
        r_in = [sem(f"r_in{q}") for q in range(GB)]
        stack_in = [sem(f"stack_in{j}") for j in range(4)]
        n1_sum, n1_mom, n1_guess, n1_step, n1_out = (sem(n) for n in ("n1_sum", "n1_mom", "n1_guess", "n1_step", "n1_out"))
        n2_sum, n2_mom, n2_guess, n2_step, n2_out = (sem(n) for n in ("n2_sum", "n2_mom", "n2_guess", "n2_step", "n2_out"))
        xT_mm, cT_mm, q_mm, k_mm, v_mm, o_mm, x2T_mm = (
            sem(n) for n in ("xT_mm", "cT_mm", "q_mm", "k_mm", "v_mm", "o_mm", "x2T_mm"))
        xT_hi, xT_lo, cT_hi, cT_lo, q_hi, q_lo, k_hi, k_lo = (
            sem(n) for n in ("xT_hi", "xT_lo", "cT_hi", "cT_lo", "q_hi", "q_lo", "k_hi", "k_lo"))
        v_out, x2_sum, x2T_out = (sem(n) for n in ("v_out", "x2_sum", "x2T_out"))
        score, maxed, expd, turned = (sem(n) for n in ("score", "maxed", "expd", "turned"))
        pT_act, pT_dve = sem("pT_act"), sem("pT_dve")
        pv = sem("pv")
        rden_out, rden_mm, o_scale, o_norm, o_hi, o_lo = (
            sem(n) for n in ("rden_out", "rden_mm", "o_scale", "o_norm", "o_hi", "o_lo"))
        res = sem("res")
        lg_mm, lg_out = sem("lg_mm"), sem("lg_out")
        r_max, r_exp, r_dve, r_t, r_tout, r_m, r_mout, r_mt, r_mtout = (
            sem(n) for n in ("r_max", "r_exp", "r_dve", "r_t", "r_tout", "r_m", "r_mout", "r_mt", "r_mtout"))
        N_RDVE = 5
        passed = sem("passed")

        block = st.enter_context(nc.Block())


        @block.sync
        def _(sp):
            def step(b, g, k):
                if has(b, -2, B - 2):
                    after(sp, xT_mm, 2 * (b + 2))
                    sp.dma_start(xt[:], x[b + 2].rearrange("(t p) n -> p t n", p=P)).then_inc(x_in, 16)
                    after(sp, cT_mm, 2 * (b + 2))
                    sp.dma_start(ct[:], ctx[b + 2].rearrange("(t p) n -> p t n", p=P)).then_inc(c_in, 16)
                if has(b, 1, B + 1):
                    q = (k - 1) % GB
                    after(sp, r_m, g - 1 if k == 0 else g)
                    sp.dma_start(x2[:, q, :, :], x[b - 1].rearrange("(t p) n -> p t n", p=P)).then_inc(r_in[q], 16)
                if has(b, -1, B - 1):
                    after(sp, q_hi, 2 * (b + 2))
                    after(sp, q_lo, 2 * (b + 2))
                    after(sp, k_hi, 2 * (b + 2))
                    after(sp, k_lo, 2 * (b + 2))
                    for j in range(4):
                        after(sp, score, H * b + 4 * j + 4)
                        for stack, first, parts in ((q_stack, 0, (0, 1, 0, 1)), (k_stack, 2, (0, 0, 1, 1))):
                            for r in range(4):
                                sp.dma_start(stack[32 * r:32 * r + 32, 4 * j:4 * j + 4, :].bitcast(F32),
                                             qk[32 * j:32 * j + 32, first + parts[r], :, :]).then_inc(stack_in[j], 16)
            run_batches(sp, step)

        @block.gpsimd
        def _(pool):
            def low_half(b, jp):
                after(pool, o_hi, 2 * b + jp + 1)
                nc.gpsimd.tensor_tensor(oT[:, 1, 2 * jp:2 * jp + 2, :], o_n[:, jp, :, :],
                                        oT[:, 0, 2 * jp:2 * jp + 2, :], ALU.subtract).then_inc(o_lo, 1)

            def step(b, g, k):
                if has(b, GB + 1, B + 2) and k == 1:
                    after(pool, r_mtout, g)
                    pool.dma_start(merged_dram[g - 1], mergedT[:]).then_inc(m_out, 16)
                if has(b, 1, B + 1):
                    q = (k - 1) % GB
                    low_half(b - 1, 1)
                    after(pool, r_in[q], 16 * (g if k == 0 else g + 1))
                    for t in range(TT):
                        last = nc.gpsimd.tensor_tensor(x2[:, q, t, :], x2[:, q, t, :], res_bias[:], ALU.add)
                    last.then_inc(res, 1)
                    after(pool, x2_sum, 2 * b)
                    pool.dma_start(out[b - 1].rearrange("(t p) n -> p t n", p=P), x2[:, q, :, :]).then_inc(x2_out, 16)
                if has(b, 0, B):
                    low_half(b, 0)
                if has(b, GB, B + 1) and k == 0:
                    after(pool, r_dve, N_RDVE * g)
                    pool.dma_start(picked_dram[g - 1], picked[:]).then_inc(p_out, 16)
            run_batches(pool, step)
            pool.wait_ge(x2_out, 16 * B)
            pool.wait_ge(m_out, 16 * NG)
            pool.wait_ge(p_out, 16 * NG)

        @block.scalar
        def _(act):
            act.preload_act_table_set("natural_log_exp_and_others")

            def norm_guess(n, mom, guess, tile):
                after(act, mom, 2 * n + 2)
                nc.scalar.activation(tile[:, 20:22], tile[:, 13:16:2], ACT.Ln, bias=eps[:]).then_inc(guess, 1)
                after(act, guess, 2 * n + 1)
                nc.scalar.activation(tile[:, 22:24], tile[:, 20:22], ACT.Exp, scale=-0.5).then_inc(guess, 1)

            def exps(b, s):
                t = H * b + s
                after(act, maxed, t + 1)
                after(act, turned, t - 1)
                if s % 8 == 0:
                    after(act, rden_out, 2 * b + s // 8 - 1)
                for q in range(TT):
                    last = nc.scalar.activation(pr[:, s % 2, q, :], S[s % 2][:, T * q:T * q + T], ACT.Exp,
                                                bias=negmax[:, s % 2, q:q + 1],
                                                accum_out=den[:, s // 8, s % 8, q:q + 1])
                last.then_inc(expd, 1)

            def take_pT(b, s):
                after(act, turned, H * b + s + 1)
                after(act, pv, 4 * b + s // 4)
                nc.scalar.activation(pT[:, s % 4, :, :].rearrange("p a t -> p (a t)"), TP[s % 2][:, :],
                                     ACT.Copy).then_inc(pT_act, 1)

            def high_half(n, i, fill, dst, sems, free):
                for f, c in free:
                    after(act, f, c)
                after(act, fill, 2 * n + i + 1)
                nc.scalar.activation(dst[:, 0, 2 * i:2 * i + 2, :].rearrange("p a t -> p (a t)"), A[i][:, :],
                                     ACT.Copy).then_inc(sems, 1)

            def step(b, g, k):
                par = (k + 1) % 2
                for s in range(H):
                    if has(b, 0, B):
                        exps(b, s)
                    s2 = s - 2
                    if s % 2 == 0 and (has(b, 0, B) if s2 >= 0 else has(b, 1, B + 1)):
                        take_pT(b if s2 >= 0 else b - 1, s2 % H)
                    prep, fin = has(b, -1, B - 1), has(b, 1, B + 1)
                    if prep and s == 0:
                        for i in range(2):
                            high_half(b + 1, i, xT_mm, xT, xT_hi, [(q_mm, 2 * (b + 1))])
                    if prep and s == 1:
                        for i in range(2):
                            high_half(b + 1, i, cT_mm, cT, cT_hi, [(v_mm, 2 * (b + 1)), (k_mm, 2 * (b + 1))])
                    if prep and s in (2, 3, 4, 5):
                        i, kind = s % 2, (s - 2) // 2
                        if i == 0 and kind == 0:
                            for j in range(4):
                                after(act, stack_in[j], 128 * (b + 1))
                        fill, done = ((q_mm, q_hi), (k_mm, k_hi))[kind]
                        after(act, fill, 2 * (b + 1) + i + 1)
                        for c in range(2):
                            bias = bqk[:, 2 if kind == 0 else 1, 2 * i + c:2 * i + c + 1]
                            last = nc.scalar.activation(qk[:, 2 * kind, 2 * i + c, :].bitcast(F32R),
                                                        A[i][:, T * c:T * c + T], ACT.Identity, bias=bias)
                        last.then_inc(done, 1)
                    if fin and s == 3:
                        attention_scale(b - 1, 1)
                    if fin and s == 4:
                        o_high(b - 1, 1)
                    if has(b, 0, B) and s == 11:
                        attention_scale(b, 0)
                    if has(b, 0, B) and s == 12:
                        o_high(b, 0)
                    if fin and s == 9:
                        norm_guess(b - 1, n2_mom, n2_guess, ln2)
                    if has(b, -2, B - 2) and s == 12:
                        norm_guess(b + 2, n1_mom, n1_guess, ln1)
                    if fin and s == 12:
                        after(act, lg_mm, b - 1)
                        for i in range(2):
                            after(act, x2T_mm, 2 * (b - 1) + i + 1)
                            nc.scalar.activation(x2T[:, 2 * i:2 * i + 2, :].rearrange("p a t -> p (a t)"), A[i][:, :],
                                                 ACT.Copy).then_inc(x2T_out, 1)
                    if fin and s == 13:
                        q = (k - 1) % GB
                        after(act, lg_mm, b)
                        if q == 0:
                            after(act, r_dve, N_RDVE * g)
                        nc.scalar.activation(lg[E * q:E * q + E, :], M[E * q:E * q + E, 0:T], ACT.Identity,
                                             bias=gb[E * q:E * q + E, :]).then_inc(lg_out, 1)
                    if has(b, GB, B + 1) and k == 0 and s == 14:
                        after(act, r_max, g)
                        nc.scalar.activation(lg[:], lg[:], ACT.Exp, bias=rt[:, 0:1], accum_out=rt[:, 1:2]).then_inc(r_exp, 1)
                    if has(b, GB + 1, B + 2) and k == 1 and s <= 2:
                        if s == 0:
                            after(act, r_t, g)
                            nc.scalar.activation(pickedT[:].rearrange("p a t -> p (a t)"), M[:, 0:TT * P],
                                                 ACT.Copy).then_inc(r_tout, 1)
                        if s == 1:
                            after(act, r_m, g)
                            nc.scalar.activation(merged[:], M[:, :], ACT.Copy).then_inc(r_mout, 1)
                        if s == 2:
                            after(act, r_mt, g)
                            after(act, m_out, 16 * (g - 1))
                            nc.scalar.activation(mergedT[:].rearrange("p a t -> p (a t)"), M[:, :],
                                                 ACT.Copy).then_inc(r_mtout, 1)
                    if prep and s >= 14:
                        i = s - 14
                        after(act, v_mm, 2 * (b + 1) + i + 1)
                        after(act, pv, 4 * b)
                        nc.scalar.activation(v[:, par, i, :], A[i][:, :], ACT.Copy).then_inc(v_out, 1)

            def attention_scale(b, jp):
                after(act, rden_mm, 2 * b + jp + 1)
                after(act, o_lo, 2 * b + jp - 1)
                nc.scalar.activation(o_n[:, jp, :, :].rearrange("p a t -> p (a t)"), M[:, :], ACT.Copy).then_inc(o_scale, 1)

            def o_high(b, jp):
                after(act, o_norm, 2 * b + jp + 1)
                after(act, o_mm, 2 * b)
                nc.scalar.activation(oT[:, 0, 2 * jp:2 * jp + 2, :], o_n[:, jp, :, :], ACT.Copy).then_inc(o_hi, 1)

            run_batches(act, step)

        @block.vector
        def _(dve):
            def norm_sums(n, src, tile, s_sum, s_mom):
                for t in range(TT):
                    nc.vector.bn_stats(tile[:, 6 * t:6 * t + 6], src[:, t, :]).then_inc(s_sum, 1)
                after_apart(dve, s_sum, 2 * n + 2, passed)
                for t in range(TT):
                    nc.vector.bn_aggr(tile[:, 12 + 2 * t:14 + 2 * t], tile[:, 6 * t:6 * t + 6]).then_inc(s_mom, 1)

            def norm_step(n, tile, guess, s_step):
                var, y, a = tile[:, 13:16:2], tile[:, 22:24], tile[:, 24:26]
                after(dve, guess, 2 * n + 2)
                nc.vector.scalar_tensor_tensor(a, var, EPS, y, ALU.add, ALU.mult).then_inc(s_step, 1)
                after(dve, s_step, 4 * n + 1)
                nc.vector.tensor_tensor(tile[:, 26:28], a, y, ALU.mult).then_inc(s_step, 1)
                after(dve, s_step, 4 * n + 2)
                nc.vector.tensor_scalar(tile[:, 28:30], tile[:, 26:28], -0.5, 1.5, ALU.mult, ALU.add).then_inc(s_step, 1)
                after(dve, s_step, 4 * n + 3)
                nc.vector.tensor_tensor(tile[:, 30:32], tile[:, 28:30], y, ALU.mult).then_inc(s_step, 1)

            def norm_apply(n, src, tile, s_step, s_out):
                after(dve, s_step, 4 * n + 4)
                for t in range(TT):
                    nc.vector.tensor_scalar(src[:, t, :], src[:, t, :], tile[:, 12 + 2 * t:13 + 2 * t],
                                            tile[:, 30 + t:31 + t], ALU.subtract, ALU.mult).then_inc(s_out, 1)

            def low_half(n, i, dst, hi, lo):
                after(dve, hi, 2 * n + i + 1)
                nc.vector.tensor_tensor(dst[:, 1, 2 * i:2 * i + 2, :].rearrange("p a t -> p (a t)"), A[i][:, :],
                                        dst[:, 0, 2 * i:2 * i + 2, :].rearrange("p a t -> p (a t)"),
                                        ALU.subtract).then_inc(lo, 1)

            def invert(b, jp):
                after(dve, expd, H * b + 8 * jp + 8)
                after(dve, rden_mm, 2 * b + jp)
                nc.vector.reciprocal(rden[:].rearrange("p q h d -> p h q d"),
                                     den[:, jp, :, :].unsqueeze(3).broadcast_to([P, H // 2, TT, DK])).then_inc(rden_out, 1)

            def normalise(b, jp):
                after(dve, pv, 4 * b + 2 * jp + 2)
                after(dve, o_scale, 2 * b + jp + 1)
                o = o_n[:, jp, :, :].rearrange("p a t -> p (a t)")
                nc.vector.tensor_tensor(o, O[:, :], o, ALU.mult).then_inc(o_norm, 1)

            def step(b, g, k):
                prep, fin = has(b, -1, B - 1), has(b, 1, B + 1)
                q = (k - 1) % GB
                for s in range(H):
                    if has(b, 0, B):
                        after(dve, score, H * b + s + 1)
                        nc.vector.reduce_max(negmax[:, s % 2, :], S[s % 2][:, :].rearrange("p (q t) -> p q t", q=TT),
                                             axis=AX.X, negate=True).then_inc(maxed, 1)
                    s2 = s - 2
                    if s % 2 == 1 and (has(b, 0, B) if s2 >= 0 else has(b, 1, B + 1)):
                        bb, hh = (b, s2) if s2 >= 0 else (b - 1, s2 % H)
                        after(dve, turned, H * bb + hh + 1)
                        after(dve, pv, 4 * bb + hh // 4)
                        nc.vector.tensor_copy(pT[:, hh % 4, :, :].rearrange("p a t -> p (a t)"),
                                              TP[hh % 2][:, :]).then_inc(pT_dve, 1)
                    if prep and s == 0:
                        for i in range(2):
                            low_half(b + 1, i, xT, xT_hi, xT_lo)
                    if prep and s == 1:
                        for i in range(2):
                            low_half(b + 1, i, cT, cT_hi, cT_lo)
                    if prep and s in (2, 3, 4, 5):
                        i, kind = s % 2, (s - 2) // 2
                        hi, lo = ((q_hi, q_lo), (k_hi, k_lo))[kind]
                        after(dve, hi, 2 * (b + 1) + i + 1)
                        for c in range(2):
                            cc = 2 * i + c
                            bias = bqk[:, 2 if kind == 0 else 1, cc:cc + 1]
                            last = nc.vector.scalar_tensor_tensor(
                                qk[:, 2 * kind + 1, cc, :].bitcast(F32R), A[i][:, T * c:T * c + T], bias,
                                qk[:, 2 * kind, cc, :], ALU.add, ALU.subtract)
                        last.then_inc(lo, 1)
                    if fin and s == 2:
                        invert(b - 1, 1)
                    if fin and s == 3:
                        normalise(b - 1, 1)
                    if has(b, 0, B) and s == 10:
                        invert(b, 0)
                    if has(b, 0, B) and s == 11:
                        normalise(b, 0)
                    if fin and s in (7, 8):
                        i = s - 7
                        after(dve, res, b)
                        after(dve, o_mm, 2 * (b - 1) + i + 1)
                        nc.vector.scalar_tensor_tensor(x2[:, q, i, :], A[i][:, :], gate[:, 1:2], x2[:, q, i, :],
                                                       ALU.mult, ALU.add).then_inc(x2_sum, 1)
                    if fin and s == 9:
                        after(dve, x2_sum, 2 * b)
                        norm_sums(b - 1, x2[:, q, :, :], ln2, n2_sum, n2_mom)
                    if fin and s == 10:
                        norm_step(b - 1, ln2, n2_guess, n2_step)
                    if fin and s == 11:
                        after(dve, x2_out, 16 * b)
                        norm_apply(b - 1, x2[:, q, :, :], ln2, n2_step, n2_out)
                    if has(b, -2, B - 2):
                        if s == 12:
                            after(dve, x_in, 16 * (b + 3))
                            norm_sums(b + 2, xt, ln1, n1_sum, n1_mom)
                        if s == 13:
                            norm_step(b + 2, ln1, n1_guess, n1_step)
                        if s == 14:
                            norm_apply(b + 2, xt, ln1, n1_step, n1_out)
                    if has(b, GB, B + 1) and k == 0 and s == 14:
                        after(dve, lg_out, b)
                        nc.vector.reduce_max(rt[:, 0:1], lg[:], axis=AX.X, negate=True).then_inc(r_max, 1)
                    if has(b, GB, B + 1) and k == 0 and s == 15:
                        done = N_RDVE * (g - 1)
                        after(dve, r_exp, g)
                        nc.vector.reciprocal(rt[:, 2:3], rt[:, 1:2]).then_inc(r_dve, 1)
                        after(dve, r_dve, done + 1)
                        nc.vector.tensor_scalar(lg[:], lg[:], rt[:, 2:3], None, ALU.mult).then_inc(r_dve, 1)
                        after_apart(dve, r_dve, done + 2, passed)
                        nc.vector.max(top8[:], lg[:]).then_inc(r_dve, 1)
                        after_apart(dve, r_dve, done + 3, passed)
                        nc.vector.match_replace(rest[:], top8[:], lg[:], 0.0).then_inc(r_dve, 1)
                        after(dve, r_dve, done + 4)
                        after(dve, p_out, 16 * (g - 1))
                        after(dve, r_t, g - 1)
                        nc.vector.tensor_tensor(picked[:], lg[:], rest[:], ALU.subtract).then_inc(r_dve, 1)
            run_batches(dve, step)

        @block.tensor
        def _(pe):
            mm, turn = nc.tensor.matmul, nc.tensor.transpose
            HALVES = ((0, 0), (0, 1), (1, 0))

            def fill_free(n, i, sems):
                for s, c in sems:
                    after(pe, s, c)

            def turn_tiles(src, i, done):
                for c in range(2):
                    for t in range(TT):
                        last = turn(A[i][:, T * c + P * t:T * c + P * t + P], src[:, t, P * (2 * i + c):P * (2 * i + c) + P],
                                    ident[:])
                last.then_inc(done, 1)

            def project_T(w, act_T, i, done):
                for c in range(2):
                    for n, (hw, ha) in enumerate(HALVES):
                        for k in range(KC):
                            last = mm(A[i][:, T * c:T * c + T], w[:, hw, k, P * (2 * i + c):P * (2 * i + c) + P],
                                      act_T[:, ha, k, :], start=(n == 0 and k == 0), stop=(n == 2 and k == KC - 1))
                last.then_inc(done, 1)

            def project(w, act_T, i, done):
                for n, (ha, hw) in enumerate(HALVES):
                    for k in range(KC):
                        last = mm(A[i][:, :], act_T[:, ha, k, P * i:P * i + P], w[:, hw, k, :],
                                  start=(n == 0 and k == 0), stop=(n == 2 and k == KC - 1))
                last.then_inc(done, 1)

            def spread(b, jp):
                after(pe, rden_out, 2 * b + jp + 1)
                for j in range(2):
                    for q in range(TT):
                        last = turn(M[:, T * j + P * q:T * j + P * q + P],
                                    rden[:, q, 4 * j:4 * j + 4, :].rearrange("p h d -> p (h d)"), ident[:])
                last.then_inc(rden_mm, 1)

            def step(b, g, k):
                prep, fin, attn = has(b, -1, B - 1), has(b, 1, B + 1), has(b, 0, B)
                q = (k - 1) % GB
                for s in range(H):
                    if attn:
                        if s % 4 == 0:
                            after(pe, stack_in[s // 4], 128 * (b + 1))
                        after(pe, expd, H * b + s - 1)
                        for qt in range(TT):
                            last = mm(S[s % 2][:, T * qt:T * qt + T], q_stack[:, s, P * qt:P * qt + P], k_stack[:, s, :],
                                      start=True, stop=True)
                        last.then_inc(score, 1)
                    s2 = s - 2
                    if has(b, 0, B) if s2 >= 0 else has(b, 1, B + 1):
                        bb, hh = (b, s2) if s2 >= 0 else (b - 1, s2 % H)
                        after(pe, expd, H * bb + hh + 1)
                        after(pe, pT_dve if hh % 2 else pT_act, 8 * bb + hh // 2)
                        for kt in range(TT):
                            for qt in range(TT):
                                last = turn(TP[hh % 2][:, T * kt + P * qt:T * kt + P * qt + P],
                                            pr[:, hh % 2, qt, P * kt:P * kt + P], ident[:])
                        last.then_inc(turned, 1)
                    s6 = s - 6
                    if s6 % 4 == 0 and (has(b, 0, B) if s6 >= 0 else has(b, 1, B + 1)):
                        bb, j = (b, s6 // 4) if s6 >= 0 else (b - 1, 3)
                        after(pe, pT_act, 8 * bb + 2 * j + 2)
                        after(pe, pT_dve, 8 * bb + 2 * j + 2)
                        after(pe, v_out, 2 * (bb + 1))
                        after(pe, o_norm, 2 * bb + j // 2)
                        vp = (k if s6 >= 0 else k - 1) % 2
                        for kt in range(TT):
                            for c in range(4):
                                last = mm(O[32 * c:32 * c + 32, T * (j % 2):T * (j % 2) + T],
                                          v[:, vp, kt, DK * (4 * j + c):DK * (4 * j + c) + DK], pT[:, c, kt, :],
                                          start=(kt == 0), stop=(kt == TT - 1), skip_group_check=True)
                        last.then_inc(pv, 1)
                    if has(b, GB + 1, B + 2) and k == 1 and s <= 2:
                        if s == 0:
                            after(pe, r_dve, N_RDVE * g)
                            after(pe, lg_out, GB * g)
                            for t in range(TT):
                                last = turn(M[:, P * t:P * t + P], picked[:, P * t:P * t + P], ident[:])
                            last.then_inc(r_t, 1)
                        if s == 1:
                            after(pe, r_tout, g)
                            for t in range(TT):
                                for kk in range(GB):
                                    last = mm(M[E * kk:E * kk + E, :], pickedT[:, t, E * kk:E * kk + E], x2[:, kk, t, :],
                                              start=(t == 0), stop=(t == TT - 1), skip_group_check=True)
                            last.then_inc(r_m, 1)
                        if s == 2:
                            after(pe, r_mout, g)
                            for c in range(KC):
                                last = turn(M[:, P * c:P * c + P], merged[:, P * c:P * c + P], ident[:])
                            last.then_inc(r_mt, 1)
                    if prep and s == 0:
                        after(pe, n1_out, 2 * (b + 2))
                        for i in range(2):
                            after(pe, v_out, 2 * b + i + 1)
                            turn_tiles(xt, i, xT_mm)
                    if prep and s == 1:
                        after(pe, c_in, 16 * (b + 2))
                        for i in range(2):
                            after(pe, xT_lo, 2 * (b + 1) + i + 1)
                            turn_tiles(ct, i, cT_mm)
                    if prep and s in (2, 3):
                        i = s - 2
                        after(pe, cT_lo, 2 * (b + 1) + i + 1)
                        after(pe, xT_lo, 2 * (b + 2))
                        project_T(w_q, xT, i, q_mm)
                    if fin and s == 3:
                        if k == 1:
                            after(pe, r_mtout, g)
                        after(pe, lg_out, b - 1)
                        after(pe, o_scale, 2 * (b - 1) + 1)
                        spread(b - 1, 1)
                    if prep and s in (4, 5):
                        i = s - 4
                        after(pe, q_lo, 2 * (b + 1) + i + 1)
                        after(pe, cT_lo, 2 * (b + 2))
                        project_T(w_k, cT, i, k_mm)
                    if fin and s in (7, 8):
                        i = s - 7
                        if prep:
                            after(pe, k_lo, 2 * (b + 1) + i + 1)
                        else:
                            after(pe, v_out, 2 * B)
                            after(pe, x2T_out, 2 * (b - 1))
                        after(pe, o_lo, 2 * b)
                        project(w_o, oT, i, o_mm)
                    if attn and s == 11:
                        after(pe, o_scale, 2 * b)
                        after(pe, r_mtout, g if k >= 1 else g - 1)
                        spread(b, 0)
                    if fin and s == 12:
                        after(pe, n2_out, 2 * b)
                        for i in range(2):
                            after(pe, x2_sum, 2 * (b - 1) + i + 1)
                            turn_tiles(x2[:, q, :, :], i, x2T_mm)
                    if fin and s == 13:
                        after(pe, x2T_out, 2 * b)
                        after(pe, o_scale, 2 * b + 1 if attn else 2 * b)
                        for c in range(KC):
                            last = mm(M[E * q:E * q + E, 0:T], gwT[:, c, :], x2T[:, c, :], start=(c == 0),
                                      stop=(c == KC - 1))
                        last.then_inc(lg_mm, 1)
                    if prep and s >= 14:
                        i = s - 14
                        after(pe, k_lo, 2 * (b + 1) + i + 1)
                        if fin:
                            after(pe, x2T_out, 2 * (b - 1) + i + 1)
                        project(w_v, cT, i, v_mm)
            run_batches(pe, step)


SLOTS = 16
PER = KC + HID // D
HC = HID // D


def experts(nc, w1, w2, merged_dram, outs_dram):
    st = ExitStack()
    with st:
        sb = lambda name, shape, dt=F32: st.enter_context(nc.sbuf_tensor(name, shape, dt))
        ps = lambda name: st.enter_context(nc.psum_tensor(name, [P, 512], F32))
        sem = lambda name: st.enter_context(nc.semaphore(name))
        ring = sb("ring", [P, SLOTS, HID])
        m_raw = sb("m_raw", [P, NG, KC, GB, E])
        m = sb("m", [P, 2, KC, B])
        w1b = sb("w1b", [1, 2, HID])
        w2b = sb("w2b", [1, 2, D])
        h = sb("h", [P, 2, D])
        hT = sb("hT", [P, 2, KC, P])
        part = sb("part", [P, 2, D])
        o = sb("o", [B, 2, D])
        ident = sb("ident2", [P, P])
        fold = sb("fold", [P, B])
        ones = sb("ones2", [1, B])
        HP = [ps("HP0"), ps("HP1")]
        TPh = [ps("TPh0"), ps("TPh1")]
        OP = [ps("OP0"), ps("OP1")]
        FP = [ps("FP0"), ps("FP1")]
        piece_in = [sem(f"piece_in{i}") for i in range(SLOTS)]
        bias_in = [sem("bias_in0"), sem("bias_in1")]
        m_in, m_out, const, h_mm, h_out, t_mm, t_out, o_mm, o_out, f_mm, f_out = (
            sem(n) for n in ("fm_in", "fm_out", "fconst", "h_mm", "h_out", "t_mm", "t_out", "fo_mm", "fo_out", "f_mm", "f_out"))
        stored = [sem("stored0"), sem("stored1")]
        block = st.enter_context(nc.Block())
        NP = E // 2

        @block.sync
        def _(sp):
            sp.dma_start(m_raw[:].rearrange("p g c k e -> p g (c k e)"), merged_dram.rearrange("g p c n -> p g (c n)")).then_inc(m_in, 16)

            def expert(e, n, first):
                for i in range(PER):
                    if not first:
                        after(sp, h_mm if i < KC else o_mm, e - 1)
                    slot = PER * n + i
                    if i < KC:
                        src = w1[e, P * i:P * i + P, :]
                    else:
                        c = i - KC
                        src = w2[e, D * c:D * c + D, :].rearrange("(p s) n -> p (s n)", p=P)
                    sp.dma_start(ring[:, slot, :], src).then_inc(piece_in[slot], 16)
            expert(0, 0, True)
            expert(1, 1, True)
            with sp.Fori(1, NP) as i:
                expert(i * 2, 0, False)
                expert(i * 2 + 1, 1, False)

        @block.gpsimd
        def _(pool):
            pool.memset(ident[:], 0.0).then_inc(const, 1)
            pool.memset(ones[:], 1.0).then_inc(const, 1)
            pool.wait_ge(const, 2)
            pool.affine_select(out=ident[:], in_=ident[:], compare_op=ALU.not_equal, fill=1.0, base=0,
                               pattern=[[-1, P]], channel_multiplier=1).then_inc(const, 1)
            pool.memset(fold[:], 0.0).then_inc(const, 1)
            pool.wait_ge(const, 4)
            for c in range(HC):
                pool.affine_select(out=fold[:], in_=fold[:], compare_op=ALU.not_equal, fill=1.0, base=-B * c,
                                   pattern=[[-1, B]], channel_multiplier=1).then_inc(const, 1)
                pool.wait_ge(const, 5 + c)

            def biases(e, n, first):
                if not first:
                    after(pool, o_mm, e - 1)
                pool.dma_start(w1b[:, n, :], w1[e, D:D + 1, :]).then_inc(bias_in[n], 16)
                pool.dma_start(w2b[:, n, :], w2[e, HID:HID + 1, :]).then_inc(bias_in[n], 16)

            def store(e, n):
                after(pool, f_out, e + 1)
                pool.dma_start(outs_dram[e], o[:, n, :]).then_inc(stored[n], 16)
            biases(0, 0, True)
            biases(1, 1, True)
            with pool.Fori(1, NP) as i:
                for n in range(2):
                    store(i * 2 + n - 2, n)
                    biases(i * 2 + n, n, False)
            store(E - 2, 0)
            store(E - 1, 1)
            for n in range(2):
                pool.wait_ge(stored[n], 16 * NP)

        @block.scalar
        def _(act):
            def expert(e, n, i):
                after(act, h_mm, e + 1)
                after(act, t_mm, e - 1)
                nc.scalar.activation(h[:, n, :], HP[n][:, :], ACT.Gelu).then_inc(h_out, 1)
                after(act, f_mm, e + 1)
                after(act, stored[n], i * 16)
                nc.scalar.activation(o[:, n, :], FP[n][0:B, :], ACT.Copy).then_inc(f_out, 1)
            expert(0, 0, 0)
            expert(1, 1, 0)
            with act.Fori(1, NP) as i:
                expert(i * 2, 0, i)
                expert(i * 2 + 1, 1, i)

        @block.vector
        def _(dve):
            dve.wait_ge(m_in, 16)

            def expert(e, n):
                after(dve, h_mm, e - 1)
                nc.vector.tensor_copy(m[:, n, :, :].rearrange("p c (k g) -> p c k g", k=GB),
                                      m_raw[:, :, :, :, e].rearrange("p g c k -> p c k g")).then_inc(m_out, 1)
                after(dve, t_mm, e + 1)
                after(dve, o_mm, e - 1)
                nc.vector.tensor_copy(hT[:, n, :, :].rearrange("p s m -> p (s m)"), TPh[n][:, :]).then_inc(t_out, 1)
                after(dve, o_mm, e + 1)
                after(dve, f_mm, e - 1)
                nc.vector.tensor_copy(part[:, n, :], OP[n][:, :]).then_inc(o_out, 1)
            expert(0, 0)
            expert(1, 1)
            with dve.Fori(1, NP) as i:
                expert(i * 2, 0)
                expert(i * 2 + 1, 1)

        @block.tensor
        def _(pe):
            mm, turn = nc.tensor.matmul, nc.tensor.transpose
            pe.wait_ge(const, 4 + HC)

            def expert(e, n, i):
                after(pe, m_out, e + 1)
                after(pe, h_out, e - 1)
                after(pe, bias_in[n], 32 * i + 32)
                for k in range(KC):
                    after(pe, piece_in[PER * n + k], 16 * i + 16)
                    for c in range(HC):
                        last = mm(HP[n][B * c:B * c + B, :], m[:, n, k, :], ring[:, PER * n + k, D * c:D * c + D],
                                  start=(k == 0), stop=False, skip_group_check=True)
                for c in range(HC):
                    last = mm(HP[n][B * c:B * c + B, :], ones[:], w1b[:, n, D * c:D * c + D], start=False, stop=True,
                              skip_group_check=True)
                last.then_inc(h_mm, 1)
                after(pe, h_out, e + 1)
                after(pe, t_out, e - 1)
                for s in range(KC):
                    last = turn(TPh[n][:, P * s:P * s + P], h[:, n, s:D:KC], ident[:])
                last.then_inc(t_mm, 1)
                after(pe, t_out, e + 1)
                after(pe, o_out, e - 1)
                for c in range(HC):
                    after(pe, piece_in[PER * n + KC + c], 16 * i + 16)
                for s in range(KC):
                    for c in range(HC):
                        last = mm(OP[n][B * c:B * c + B, :], hT[:, n, s, B * c:B * c + B],
                                  ring[:, PER * n + KC + c, D * s:D * s + D], start=(s == 0), stop=(s == KC - 1 and c > 0),
                                  skip_group_check=True)
                last = mm(OP[n][0:B, :], ones[:], w2b[:, n, :], start=False, stop=True, skip_group_check=True)
                last.then_inc(o_mm, 1)
                after(pe, o_out, e + 1)
                after(pe, f_out, e - 1)
                mm(FP[n][0:B, :], fold[:], part[:, n, :], start=True, stop=True).then_inc(f_mm, 1)

            expert(0, 0, 0)
            expert(1, 1, 0)
            with pe.Fori(1, NP) as i:
                expert(i * 2, 0, i)
                expert(i * 2 + 1, 1, i)


def combine(nc, g_ffn, out, picked_dram, outs_dram):
    st = ExitStack()
    with st:
        sb = lambda name, shape, dt=F32: st.enter_context(nc.sbuf_tensor(name, shape, dt))
        sem = lambda name: st.enter_context(nc.semaphore(name))
        o = sb("o_all", [P, NG, D])
        xr = sb("xr", [P, 2, GB, TT, D])
        pz = sb("pz", [P, 2, GB, T])
        gate = sb("gate_f", [P, 2])
        Y = [st.enter_context(nc.psum_tensor(f"Y{i}", [P, D], F32)) for i in range(8)]
        N = 2 * GB
        x_in = [sem(f"x_in_f{i}") for i in range(N)]
        p_in = [sem(f"p_in_f{i}") for i in range(N)]
        x_out = [sem(f"x_out_f{i}") for i in range(N)]
        o_in, g_in, gated, zeroed, y_mm, y_sum = (sem(n) for n in ("o_in_f", "g_in_f", "gated", "zeroed", "y_mm", "y_sum"))
        block = st.enter_context(nc.Block())

        def turns(eng, turn):
            turn(0)
            with eng.Fori(1, B // N) as i:
                turn(i)

        @block.sync
        def _(sp):
            sp.dma_start(gate[:, 0:1], g_ffn.rearrange("(a n) -> a n", a=1).broadcast_to([P, 1])).then_inc(g_in, 16)
            for k in range(GB):
                sp.dma_start(o[E * k:E * k + E, :, :], outs_dram[:, NG * k:NG * k + NG, :]).then_inc(o_in, 16)
            sp.wait_ge(zeroed, 1)

            def turn(i):
                for n in range(N):
                    k = n % GB
                    after(sp, y_mm, i * 2 * N + 2 * (n + 1) - 2 * N)
                    sp.dma_start(pz[E * k:E * k + E, n // GB, k, :],
                                 picked_dram[i * 2 + n // GB, E * k:E * k + E, :]).then_inc(p_in[n], 16)
                    after(sp, x_out[n], i * 16)
                    sp.dma_start(xr[:, n // GB, k, :, :], out[i * N + n].rearrange("(t p) n -> p t n", p=P)).then_inc(x_in[n], 16)
            turns(sp, turn)

        @block.scalar
        def _(act):
            act.wait_ge(g_in, 16)
            act.activation(gate[:, 1:2], gate[:, 0:1], ACT.Tanh).then_inc(gated, 1)

            def turn(i):
                for n in range(N):
                    after(act, y_sum, i * 2 * N + 2 * (n + 1))
                    act.dma_start(out[i * N + n].rearrange("(t p) n -> p t n", p=P), xr[:, n // GB, n % GB, :, :]).then_inc(x_out[n], 16)
            turns(act, turn)
            for n in range(N):
                act.wait_ge(x_out[n], 16 * (B // N))

        @block.vector
        def _(dve):
            dve.memset(pz[:], 0.0).then_inc(zeroed, 1)
            dve.wait_ge(gated, 1)

            def turn(i):
                for n in range(N):
                    after(dve, x_in[n], i * 16 + 16)
                    for t in range(TT):
                        after(dve, y_mm, i * 2 * N + 2 * n + t + 1)
                        x_t = xr[:, n // GB, n % GB, t, :]
                        nc.vector.scalar_tensor_tensor(x_t, Y[(2 * n + t) % 8][:, :], gate[:, 1:2], x_t, ALU.mult,
                                                       ALU.add).then_inc(y_sum, 1)
            turns(dve, turn)

        @block.tensor
        def _(pe):
            pe.wait_ge(o_in, 16 * GB)

            def turn(i):
                for n in range(N):
                    after(pe, p_in[n], i * 16 + 16)
                    for t in range(TT):
                        after(pe, y_sum, i * 2 * N + 2 * n + t + 1 - 8)
                        nc.tensor.matmul(Y[(2 * n + t) % 8][:, :], pz[:, n // GB, n % GB, P * t:P * t + P],
                                         o[:, i * 2 + n // GB, :], start=True, stop=True).then_inc(y_mm, 1)
            turns(pe, turn)


def build(nc, A, out):
    merged_dram = nc.dram_tensor("merged_scratch", [NG, P, KC, P], F32, kind="Internal").ap()
    picked_dram = nc.dram_tensor("picked_scratch", [NG, P, T], F32, kind="Internal").ap()
    outs_dram = nc.dram_tensor("outs_scratch", [E, B, D], F32, kind="Internal").ap()
    attention_and_routing(nc, A["x"], A["ctx_1024"], A["g_xattn"], A["L0_xattn_Wq"], A["L0_xattn_bq"], A["L0_xattn_Wk"],
                          A["L0_xattn_bk"], A["L0_xattn_Wv"], A["L0_xattn_bv"], A["L0_xattn_Wo"], A["L0_xattn_bo"],
                          A["L0_ffn_gate_w"], A["L0_ffn_gate_b"], out, merged_dram, picked_dram)
    experts(nc, A["L0_ffn_w1"], A["L0_ffn_w2"], merged_dram, outs_dram)
    combine(nc, A["g_ffn"], out, picked_dram, outs_dram)


def kernel(**inputs):
    import concourse.bacc as bacc
    from concourse.bass_utils import run_bass_kernel_spmd

    nc = bacc.Bacc("TRN2", target_bir_lowering=False, num_devices=1)
    arrays, aps = {}, {}
    for name, a in inputs.items():
        a = np.ascontiguousarray(a)
        arrays[name + "_in"] = a
        aps[name] = nc.dram_tensor(name + "_in", a.shape, mybir.dt.from_np(a.dtype), kind="ExternalInput").ap()
    out = nc.dram_tensor("y_out", [B, T, D], F32, kind="ExternalOutput").ap()
    build(nc, aps, out)
    return run_bass_kernel_spmd(nc, [arrays], core_ids=[0]).results[0]["y_out"]
```

```python
from contextlib import ExitStack

import numpy as np

import concourse.bass as bass
from concourse import mybir
from concourse.alu_op_type import AluOpType as ALU

F32 = mybir.dt.float32
F32R = mybir.dt.float32r
ACT = mybir.ActivationFunctionType
AX = mybir.AxisListType

B, T, D = 32, 256, 512
H, DK = 16, 32
E, HID, TOP = 32, 2048, 8
P = 128
KC = D // P
TT = T // P
GB = 4
NG = B // GB
HB = H // 4
SCALE = float(DK) ** -0.5
EPS = 1e-5


def after(eng, sem, count):
    if isinstance(count, int) and count <= 0:
        return
    eng.wait_ge(sem, count)


def after_apart(eng, sem, count, passed):
    if isinstance(count, int) and count <= 0:
        return
    eng.wait_ge(sem, count)
    eng.sem_inc(passed, 1)


def run_batches(eng, step):
    for b in range(-2, 2 * GB):
        step(b, b // GB, b % GB)
    with eng.Fori(2, NG - 1) as g:
        for k in range(GB):
            step(g * GB + k, g, k)
    for b in range(B - GB, B + 2):
        step(b, b // GB, b % GB)


def has(b, low, high):
    return low <= b < high if isinstance(b, int) else True


def attention_and_routing(nc, x, ctx, g_xattn, wq, bq, wk, bk, wv, bv, wo, bo, gate_w, gate_b, out, merged_dram,
                          picked_dram):
    st = ExitStack()
    with st:
        sb = lambda name, shape, dt=F32: st.enter_context(nc.sbuf_tensor(name, shape, dt))
        ps = lambda name: st.enter_context(nc.psum_tensor(name, [P, 512], F32))
        sem = lambda name: st.enter_context(nc.semaphore(name))

        w_q, w_k, w_v, w_o = (sb(n, [P, 2, KC, D], F32R) for n in ("w_q", "w_k", "w_v", "w_o"))
        q_stack = sb("q_stack", [P, H, T], F32R)
        k_stack = sb("k_stack", [P, H, T], F32R)
        xt = sb("xt", [P, TT, D])
        ct = sb("ct", [P, TT, D])
        xT = sb("xT", [P, 2, KC, T], F32R)
        cT = sb("cT", [P, 2, KC, T], F32R)
        qk = sb("qk", [P, 4, HB, T])
        v = sb("v", [P, 2, TT, D])
        pr = sb("pr", [P, 2, TT, T])
        pT = sb("pT", [P, 4, TT, T])
        den = sb("den", [P, 2, H // 2, TT])
        rden = sb("rden", [P, TT, H // 2, DK])
        rs = sb("rs", [P, H // 2, TT])
        negmax = sb("negmax", [P, 2, TT])
        o_n = sb("o_n", [P, 2, 2, T])
        oT = sb("oT", [P, 2, KC, T], F32R)
        x2 = sb("x2", [P, GB, TT, D])
        x2T = sb("x2T", [P, KC, T])
        lg = sb("lg", [P, T])
        picked = sb("picked", [P, T])
        pickedT = sb("pickedT", [P, TT, P])
        merged = sb("merged", [P, D])
        mergedT = sb("mergedT", [P, KC, P])
        top8 = sb("top8", [P, TOP])
        rt = sb("rt", [P, 4])
        ln1 = sb("ln1", [P, 32])
        ln2 = sb("ln2", [P, 32])
        ident = sb("ident", [P, P])
        ones = sb("ones", [1, P])
        bv_col = sb("bv_col", [P, KC])
        res_bias = sb("res_bias", [P, D])
        bqk = sb("bqk", [P, 3, HB])
        gwT = sb("gwT", [P, KC, E])
        gb = sb("gb", [P, 1])
        gate = sb("gate", [P, 2])
        eps = sb("eps", [P, 1])

        S = [ps("S0"), ps("S1")]
        TP = [ps("TP0"), ps("TP1")]
        A = [ps("A0"), ps("A1")]
        O = ps("O")
        M = ps("M")

        load = [sem(f"load_{n}") for n in ("wq", "wk", "wv", "wo")]
        small, const, split_hi, split_lo, setup_mm, setup_v, setup_a = (
            sem(n) for n in ("small", "const", "split_hi", "split_lo", "setup_mm", "setup_v", "setup_a"))
        bv_wide = ct[:, 0, :].rearrange("p (k m) -> p k m", k=KC)
        bo_row, gw = ct[0:1, 1, :], xt[0:E, 0, :]
        raw = [qk[:, 2 * i:2 * i + 2, :, :].rearrange("p a c t -> p (a c t)").rearrange("p (k n) -> p k n", k=KC)
               for i in range(2)]
        raw += [x2[:, 2 * i:2 * i + 2, :, :].rearrange("p a c t -> p (a c t)").rearrange("p (k n) -> p k n", k=KC)
                for i in range(2)]
        weights = [w_q, w_k, w_v, w_o]

        def pieces(i, k):
            if i >= 2:
                return [(raw[i][:, k, :], [weights[i][:, half, k, :] for half in range(2)])]
            src = raw[i][:, k, :].rearrange("p (j c d) -> p c j d", j=4, c=4)
            return [(src[:, c], [weights[i][:, half, k, P * c:P * c + P].rearrange("p (j d) -> p j d", j=4)
                                 for half in range(2)]) for c in range(4)]

        n_small = 8 + 2 + 4 + 2
        with nc.Block() as block:

            @block.sync
            def _(sp):
                for i, w in enumerate((wq, wk, wv, wo)):
                    sp.dma_start(raw[i], w.rearrange("(k p) n -> p k n", p=P)).then_inc(load[i], 16)

            @block.gpsimd
            def _(pool):
                for i, bias in enumerate((bq, bk)):
                    for j in range(4):
                        pool.dma_start(bqk[32 * j:32 * j + 32, i, :],
                                       bias[P * j:P * j + P].rearrange("(c d) -> d c", d=DK),
                                       allow_slow_non_contiguous=True).then_inc(small, 16)
                pool.dma_start(bv_col[:], bv.rearrange("(k p) -> p k", p=P),
                               allow_slow_non_contiguous=True).then_inc(small, 16)
                pool.dma_start(bo_row, bo.rearrange("(a n) -> a n", a=1)).then_inc(small, 16)
                for j in range(GB):
                    pool.dma_start(gb[E * j:E * j + E, :], gate_b.rearrange("(e a) -> e a", a=1)).then_inc(small, 16)
                pool.dma_start(gw, gate_w).then_inc(small, 16)
                pool.dma_start(gate[:, 0:1], g_xattn.rearrange("(a n) -> a n", a=1).broadcast_to([P, 1])).then_inc(small, 16)
                pool.memset(ident[:], 0.0).then_inc(const, 1)
                pool.wait_ge(const, 1)
                pool.affine_select(out=ident[:], in_=ident[:], compare_op=ALU.not_equal, fill=1.0, base=0,
                                   pattern=[[-1, P]], channel_multiplier=1).then_inc(const, 1)
                pool.memset(ones[:], 1.0).then_inc(const, 1)
                pool.memset(eps[:], EPS).then_inc(const, 1)

            @block.scalar
            def _(act):
                for i in range(4):
                    act.wait_ge(load[i], 16)
                    for k in range(KC):
                        for src, dst in pieces(i, k):
                            last = act.activation(dst[0], src, ACT.Copy, scale=SCALE if i == 0 else 1.0)
                        last.then_inc(split_hi, 1)
                act.wait_ge(small, 16 * n_small)
                act.activation(gate[:, 1:2], gate[:, 0:1], ACT.Tanh).then_inc(setup_a, 1)
                act.wait_ge(setup_a, 1)
                act.wait_ge(setup_mm, 1)
                act.activation(res_bias[:], A[0][:, :], ACT.Copy, scale=gate[:, 1:2]).then_inc(setup_a, 1)
                act.wait_ge(setup_mm, 2)
                act.activation(gwT[:].rearrange("p k e -> p (k e)"), A[1][:, 0:KC * E], ACT.Copy).then_inc(setup_a, 1)

            @block.vector
            def _(dve):
                dve.wait_ge(small, 16 * n_small)
                dve.tensor_scalar(bqk[:, 2, :], bqk[:, 0, :], SCALE, None, ALU.mult).then_inc(setup_v, 1)
                for k in range(KC):
                    dve.tensor_copy(bv_wide[:, k, :], bv_col[:, k:k + 1].broadcast_to([P, P])).then_inc(setup_v, 1)
                for i in range(4):
                    dve.wait_ge(load[i], 16)
                    for k in range(KC):
                        dve.wait_ge(split_hi, KC * i + k + 1)
                        for src, dst in pieces(i, k):
                            last = dve.scalar_tensor_tensor(dst[1], src, SCALE if i == 0 else 1.0, dst[0], ALU.mult,
                                                            ALU.subtract)
                        last.then_inc(split_lo, 1)

            @block.tensor
            def _(pe):
                pe.wait_ge(setup_v, 1 + KC)
                pe.wait_ge(const, 4)
                pe.wait_ge(load[3], 16)
                pe.wait_ge(small, 16 * n_small)
                for k in range(KC):
                    nc.tensor.matmul(A[0][:, :], bv_wide[:, k, :], raw[3][:, k, :], start=(k == 0), stop=False)
                nc.tensor.matmul(A[0][:, :], ones[:], bo_row, start=False, stop=True).then_inc(setup_mm, 1)
                for k in range(KC):
                    last = nc.tensor.transpose(A[1][:, E * k:E * k + E], gw[:, P * k:P * k + P], ident[0:E, 0:E])
                last.then_inc(setup_mm, 1)

        x_in, c_in, x2_out, m_out, p_out = (sem(n) for n in ("x_in", "c_in", "x2_out", "m_out", "p_out"))
        r_in = [sem(f"r_in{q}") for q in range(GB)]
        q_in = [sem(f"q_in{j}") for j in range(4)]
        k_in = [sem(f"k_in{j}") for j in range(4)]
        n1_sum, n1_mom, n1_guess, n1_step, n1_out = (sem(n) for n in ("n1_sum", "n1_mom", "n1_guess", "n1_step", "n1_out"))
        n2_sum, n2_mom, n2_guess, n2_step, n2_out = (sem(n) for n in ("n2_sum", "n2_mom", "n2_guess", "n2_step", "n2_out"))
        xT_mm, cT_mm, q_mm, k_mm, v_mm, o_mm, x2T_mm = (
            sem(n) for n in ("xT_mm", "cT_mm", "q_mm", "k_mm", "v_mm", "o_mm", "x2T_mm"))
        xT_hi, xT_lo, cT_hi, cT_lo, q_hi, q_lo, k_hi, k_lo = (
            sem(n) for n in ("xT_hi", "xT_lo", "cT_hi", "cT_lo", "q_hi", "q_lo", "k_hi", "k_lo"))
        v_out, x2_sum, x2T_out = (sem(n) for n in ("v_out", "x2_sum", "x2T_out"))
        score, maxed, expd, turned = (sem(n) for n in ("score", "maxed", "expd", "turned"))
        pT_act, pT_dve = sem("pT_act"), sem("pT_dve")
        pv = sem("pv")
        rsum, rden_out, rden_mm, o_scale, o_norm, o_hi, o_lo = (
            sem(n) for n in ("rsum", "rden_out", "rden_mm", "o_scale", "o_norm", "o_hi", "o_lo"))
        res = sem("res")
        lg_mm, lg_out = sem("lg_mm"), sem("lg_out")
        r_max, r_exp, r_dve, r_t, r_tout, r_m, r_mout, r_mt, r_mtout = (
            sem(n) for n in ("r_max", "r_exp", "r_dve", "r_t", "r_tout", "r_m", "r_mout", "r_mt", "r_mtout"))
        N_RDVE = 5
        passed, passed_pool = sem("passed"), sem("passed_pool")

        block = st.enter_context(nc.Block())


        @block.sync
        def _(sp):
            def fill_stack(j, stack, first, parts, done):
                for r in range(4):
                    sp.dma_start(stack[32 * r:32 * r + 32, 4 * j:4 * j + 4, :].bitcast(F32),
                                 qk[32 * j:32 * j + 32, first + parts[r], :, :]).then_inc(done, 16)

            def load(dst, src, done):
                sp.dma_start(dst[:], src.rearrange("(t p) n -> p t n", p=P)).then_inc(done, 16)

            def step(b, g, k):
                prep = has(b, -1, B - 1)
                if prep:
                    after(sp, q_lo, 2 * (b + 2))
                    for j in range(2):
                        after(sp, score, H * b + 4 * j + 4)
                        fill_stack(j, q_stack, 0, (0, 1, 0, 1), q_in[j])
                if has(b, -2, B - 2):
                    after(sp, cT_mm, 2 * (b + 2))
                    load(ct, ctx[b + 2], c_in)
                if prep:
                    after(sp, score, H * b + 12)
                    fill_stack(2, q_stack, 0, (0, 1, 0, 1), q_in[2])
                if has(b, -2, B - 3):
                    after(sp, xT_mm, 2 * (b + 3))
                    load(xt, x[b + 3], x_in)
                if prep:
                    after(sp, k_lo, 2 * (b + 2))
                    for j in range(3):
                        fill_stack(j, k_stack, 2, (0, 0, 1, 1), k_in[j])
                    after(sp, score, H * b + H)
                    fill_stack(3, q_stack, 0, (0, 1, 0, 1), q_in[3])
                    fill_stack(3, k_stack, 2, (0, 0, 1, 1), k_in[3])
            load(xt, x[0], x_in)
            run_batches(sp, step)

        @block.gpsimd
        def _(pool):
            def load_again(n, q, merged_groups):
                after_apart(pool, r_m, merged_groups, passed_pool)
                pool.dma_start(x2[:, q, :, :], x[n].rearrange("(t p) n -> p t n", p=P)).then_inc(r_in[q], 16)

            def step(b, g, k):
                routing = has(b, GB + 1, B + 2) and k == 1
                if routing:
                    after_apart(pool, r_dve, N_RDVE * g, passed_pool)
                    pool.dma_start(picked_dram[g - 1], picked[:]).then_inc(p_out, 16)
                if has(b, 1, B + 1):
                    q = (k - 1) % GB
                    if k == 1:
                        load_again(b - 1, q, g)
                    after(pool, r_in[q], 16 * (g if k == 0 else g + 1))
                    for t in range(TT):
                        last = nc.gpsimd.tensor_tensor(x2[:, q, t, :], x2[:, q, t, :], res_bias[:], ALU.add)
                    last.then_inc(res, 1)
                    after_apart(pool, x2_sum, 2 * b, passed_pool)
                    pool.dma_start(out[b - 1].rearrange("(t p) n -> p t n", p=P), x2[:, q, :, :]).then_inc(x2_out, 16)
                if has(b, 1, B) and k != 0:
                    load_again(b, k, g)
                if routing:
                    after_apart(pool, r_mtout, g, passed_pool)
                    pool.dma_start(merged_dram[g - 1], mergedT[:]).then_inc(m_out, 16)
            run_batches(pool, step)
            pool.wait_ge(x2_out, 16 * B)
            pool.wait_ge(m_out, 16 * NG)
            pool.wait_ge(p_out, 16 * NG)

        @block.scalar
        def _(act):
            act.preload_act_table_set("natural_log_exp_and_others")

            def copy(dst, src):
                return nc.scalar.activation(dst, src, ACT.Copy)

            def norm_guess(n, mom, guess, tile):
                after(act, mom, 2 * n + 2)
                nc.scalar.activation(tile[:, 20:22], tile[:, 13:16:2], ACT.Ln, bias=eps[:]).then_inc(guess, 1)
                after(act, guess, 2 * n + 1)
                nc.scalar.activation(tile[:, 22:24], tile[:, 20:22], ACT.Exp, scale=-0.5).then_inc(guess, 1)

            def exps(b, s):
                t = H * b + s
                after(act, maxed, t + 1)
                after(act, turned, t - 1)
                if s % 8 == 0:
                    after(act, rsum, 2 * b + s // 8 - 1)
                for q in range(TT):
                    last = nc.scalar.activation(pr[:, s % 2, q, :], S[s % 2][:, T * q:T * q + T], ACT.Exp,
                                                bias=negmax[:, s % 2, q:q + 1],
                                                accum_out=den[:, s // 8, s % 8, q:q + 1])
                last.then_inc(expd, 1)

            def take_pT(b, s):
                after(act, turned, H * b + s + 1)
                after(act, pv, 4 * b + s // 4)
                copy(pT[:, s % 4, :, :].rearrange("p a t -> p (a t)"), TP[s % 2][:, :]).then_inc(pT_act, 1)

            def high_half_qk(b, i, kind):
                fill, done = ((q_mm, q_hi), (k_mm, k_hi))[kind]
                if i == 0:
                    for j in range(4):
                        after(act, (q_in, k_in)[kind][j], 64 * b)
                after(act, fill, 2 * b + i + 1)
                for c in range(2):
                    bias = bqk[:, 2 if kind == 0 else 1, 2 * i + c:2 * i + c + 1]
                    last = nc.scalar.activation(qk[:, 2 * kind, 2 * i + c, :].bitcast(F32R),
                                                A[i][:, T * c:T * c + T], ACT.Identity, bias=bias)
                last.then_inc(done, 1)

            def take_v(b, i, par):
                after(act, v_mm, 2 * b + i + 1)
                after(act, pv, 4 * (b - 1))
                copy(v[:, par, i, :], A[i][:, :]).then_inc(v_out, 1)

            def scale(b, jp):
                after(act, rden_mm, 2 * b + jp + 1)
                after(act, o_lo, 2 * b + jp - 1)
                copy(o_n[:, jp, :, :].rearrange("p a t -> p (a t)"), M[:, :]).then_inc(o_scale, 1)

            def high_half_o(b, jp):
                after(act, o_norm, 2 * b + jp + 1)
                after(act, o_mm, 2 * b)
                copy(oT[:, 0, 2 * jp:2 * jp + 2, :], o_n[:, jp, :, :]).then_inc(o_hi, 1)

            def step(b, g, k):
                attn, prep, fin, ahead = has(b, 0, B), has(b, -1, B - 1), has(b, 1, B + 1), has(b, -2, B - 2)
                routing = has(b, GB + 1, B + 2) and k == 1
                for s in range(H):
                    if attn:
                        exps(b, s)
                    if s % 2 == 0 and (attn if s >= 2 else fin):
                        take_pT(b if s >= 2 else b - 1, (s - 2) % H)
                    if s == 1 and fin:
                        scale(b - 1, 1)
                    if s == 3 and routing:
                        after(act, r_t, g)
                        copy(pickedT[:].rearrange("p a t -> p (a t)"), M[:, 0:TT * P]).then_inc(r_tout, 1)
                    if s == 4 and routing:
                        after(act, r_m, g)
                        copy(merged[:], M[:, :]).then_inc(r_mout, 1)
                    if s == 5 and routing:
                        after(act, r_mt, g)
                        after(act, m_out, 16 * (g - 1))
                        copy(mergedT[:].rearrange("p a t -> p (a t)"), M[:, :]).then_inc(r_mtout, 1)
                    if s == 9 and attn:
                        scale(b, 0)
                    if s in (13, 14) and fin:
                        i = s - 13
                        after(act, lg_mm, b - 1)
                        after(act, x2T_mm, 2 * (b - 1) + i + 1)
                        copy(x2T[:, 2 * i:2 * i + 2, :].rearrange("p a t -> p (a t)"), M[:, :]).then_inc(x2T_out, 1)
                    if s == 15 and fin:
                        q = (k - 1) % GB
                        after(act, lg_mm, b)
                        if q == 0:
                            after(act, r_dve, N_RDVE * g)
                        nc.scalar.activation(lg[E * q:E * q + E, :], M[E * q:E * q + E, 0:T], ACT.Identity,
                                             bias=gb[E * q:E * q + E, :]).then_inc(lg_out, 1)
                    if s == 0 and attn:
                        take_v(b, 1, k % 2)
                    if s in (2, 4) and prep:
                        high_half_qk(b + 1, (s - 2) // 2, 0)
                    if s in (10, 12) and prep:
                        high_half_qk(b + 1, (s - 10) // 2, 1)
                    if s == 14 and prep:
                        take_v(b + 1, 0, (k + 1) % 2)
                    if s == 3 and fin:
                        high_half_o(b - 1, 1)
                    if s == 12 and attn:
                        high_half_o(b, 0)
                    if s == 2 and ahead:
                        norm_guess(b + 2, n1_mom, n1_guess, ln1)
                    if s == 9 and fin:
                        norm_guess(b - 1, n2_mom, n2_guess, ln2)
                    if s == 0 and routing:
                        after(act, r_max, g)
                        nc.scalar.activation(lg[:], lg[:], ACT.Exp, bias=rt[:, 0:1], accum_out=rt[:, 1:2]).then_inc(r_exp, 1)
            run_batches(act, step)

        @block.vector
        def _(dve):
            def norm_sums(n, t, src, tile, s_sum, s_mom):
                nc.vector.bn_stats(tile[:, 6 * t:6 * t + 6], src[:, t, :]).then_inc(s_sum, 1)
                if t == TT - 1:
                    after_apart(dve, s_sum, 2 * n + 2, passed)
                    for t in range(TT):
                        nc.vector.bn_aggr(tile[:, 12 + 2 * t:14 + 2 * t], tile[:, 6 * t:6 * t + 6]).then_inc(s_mom, 1)

            def norm_step(n, tile, guess, s_step):
                var, y, a = tile[:, 13:16:2], tile[:, 22:24], tile[:, 24:26]
                after(dve, guess, 2 * n + 2)
                nc.vector.scalar_tensor_tensor(a, var, EPS, y, ALU.add, ALU.mult).then_inc(s_step, 1)
                after(dve, s_step, 4 * n + 1)
                nc.vector.tensor_tensor(tile[:, 26:28], a, y, ALU.mult).then_inc(s_step, 1)
                after(dve, s_step, 4 * n + 2)
                nc.vector.tensor_scalar(tile[:, 28:30], tile[:, 26:28], -0.5, 1.5, ALU.mult, ALU.add).then_inc(s_step, 1)
                after(dve, s_step, 4 * n + 3)
                nc.vector.tensor_tensor(tile[:, 30:32], tile[:, 28:30], y, ALU.mult).then_inc(s_step, 1)

            def norm_apply(n, src, tile, s_step, s_out):
                after(dve, s_step, 4 * n + 4)
                for t in range(TT):
                    nc.vector.tensor_scalar(src[:, t, :], src[:, t, :], tile[:, 12 + 2 * t:13 + 2 * t],
                                            tile[:, 30 + t:31 + t], ALU.subtract, ALU.mult).then_inc(s_out, 1)

            def both_halves(n, i, dst, fill, hi, lo):
                after(dve, fill, 2 * n + i + 1)
                nc.vector.tensor_copy(dst[:, 0, 2 * i:2 * i + 2, :].rearrange("p a t -> p (a t)"), M[:, :]).then_inc(hi, 1)
                after(dve, hi, 2 * n + i + 1)
                nc.vector.tensor_tensor(dst[:, 1, 2 * i:2 * i + 2, :].rearrange("p a t -> p (a t)"), M[:, :],
                                        dst[:, 0, 2 * i:2 * i + 2, :].rearrange("p a t -> p (a t)"),
                                        ALU.subtract).then_inc(lo, 1)

            def low_half_qk(b, i, kind):
                hi, lo = ((q_hi, q_lo), (k_hi, k_lo))[kind]
                after(dve, hi, 2 * b + i + 1)
                for c in range(2):
                    cc = 2 * i + c
                    bias = bqk[:, 2 if kind == 0 else 1, cc:cc + 1]
                    last = nc.vector.scalar_tensor_tensor(
                        qk[:, 2 * kind + 1, cc, :].bitcast(F32R), A[i][:, T * c:T * c + T], bias,
                        qk[:, 2 * kind, cc, :], ALU.add, ALU.subtract)
                last.then_inc(lo, 1)

            def invert(b, jp):
                after(dve, expd, H * b + 8 * jp + 8)
                nc.vector.reciprocal(rs[:], den[:, jp, :, :]).then_inc(rsum, 1)
                after(dve, rsum, 2 * b + jp + 1)
                after(dve, rden_mm, 2 * b + jp)
                nc.vector.tensor_copy(rden[:].rearrange("p q h d -> p h q d"),
                                      rs[:].unsqueeze(3).broadcast_to([P, H // 2, TT, DK])).then_inc(rden_out, 1)

            def normalise(b, jp):
                after(dve, pv, 4 * b + 2 * jp + 2)
                after(dve, o_scale, 2 * b + jp + 1)
                o = o_n[:, jp, :, :].rearrange("p a t -> p (a t)")
                nc.vector.tensor_tensor(o, O[:, :], o, ALU.mult).then_inc(o_norm, 1)

            def low_half_o(b, jp):
                after(dve, o_hi, 2 * b + jp + 1)
                nc.vector.tensor_tensor(oT[:, 1, 2 * jp:2 * jp + 2, :], o_n[:, jp, :, :],
                                        oT[:, 0, 2 * jp:2 * jp + 2, :], ALU.subtract).then_inc(o_lo, 1)

            def step(b, g, k):
                attn, prep, fin, ahead = has(b, 0, B), has(b, -1, B - 1), has(b, 1, B + 1), has(b, -2, B - 2)
                q = (k - 1) % GB
                for s in range(H):
                    if attn:
                        after(dve, score, H * b + s + 1)
                        nc.vector.reduce_max(negmax[:, s % 2, :], S[s % 2][:, :].rearrange("p (q t) -> p q t", q=TT),
                                             axis=AX.X, negate=True).then_inc(maxed, 1)
                    if s % 2 == 1 and (attn if s >= 2 else fin):
                        bb, hh = (b if s >= 2 else b - 1), (s - 2) % H
                        after(dve, turned, H * bb + hh + 1)
                        after(dve, pv, 4 * bb + hh // 4)
                        nc.vector.tensor_copy(pT[:, hh % 4, :, :].rearrange("p a t -> p (a t)"),
                                              TP[hh % 2][:, :]).then_inc(pT_dve, 1)
                    if s in (3, 5) and prep:
                        low_half_qk(b + 1, (s - 3) // 2, 0)
                    if s in (11, 13) and prep:
                        low_half_qk(b + 1, (s - 11) // 2, 1)
                    if s in (6, 8) and fin:
                        i = (s - 6) // 2
                        after(dve, res, b)
                        after(dve, o_mm, 2 * (b - 1) + i + 1)
                        nc.vector.scalar_tensor_tensor(x2[:, q, i, :], A[i][:, :], gate[:, 1:2], x2[:, q, i, :],
                                                       ALU.mult, ALU.add).then_inc(x2_sum, 1)
                    if s in (2, 6) and prep:
                        after(dve, v_mm, 2 * (b + 1))
                        both_halves(b + 1, (s - 2) // 4, cT, cT_mm, cT_hi, cT_lo)
                    if s in (10, 12) and ahead:
                        after(dve, q_mm, 2 * (b + 2))
                        both_halves(b + 2, (s - 10) // 2, xT, xT_mm, xT_hi, xT_lo)
                    if s == 0 and fin:
                        invert(b - 1, 1)
                    if s == 2 and fin:
                        normalise(b - 1, 1)
                    if s == 4 and fin:
                        low_half_o(b - 1, 1)
                    if s == 8 and attn:
                        invert(b, 0)
                    if s == 11 and attn:
                        normalise(b, 0)
                    if s == 14 and attn:
                        low_half_o(b, 0)
                    if s in (7, 8) and fin:
                        after(dve, x2_sum, 2 * (b - 1) + s - 6)
                        norm_sums(b - 1, s - 7, x2[:, q, :, :], ln2, n2_sum, n2_mom)
                    if s == 10 and fin:
                        norm_step(b - 1, ln2, n2_guess, n2_step)
                    if s == 12 and fin:
                        after(dve, x2_out, 16 * b)
                        norm_apply(b - 1, x2[:, q, :, :], ln2, n2_step, n2_out)
                    if s in (0, 1) and ahead:
                        after(dve, x_in, 16 * (b + 3))
                        norm_sums(b + 2, s, xt, ln1, n1_sum, n1_mom)
                    if s == 4 and ahead:
                        norm_step(b + 2, ln1, n1_guess, n1_step)
                    if s == 7 and ahead:
                        norm_apply(b + 2, xt, ln1, n1_step, n1_out)
                    if s == 0 and has(b, GB + 1, B + 2) and k == 1:
                        after(dve, lg_out, b - 1)
                        nc.vector.reduce_max(rt[:, 0:1], lg[:], axis=AX.X, negate=True).then_inc(r_max, 1)
                    if s == 1 and has(b, GB + 1, B + 2) and k == 1:
                        done = N_RDVE * (g - 1)
                        after(dve, r_exp, g)
                        nc.vector.reciprocal(rt[:, 2:3], rt[:, 1:2]).then_inc(r_dve, 1)
                        after(dve, r_dve, done + 1)
                        nc.vector.tensor_scalar(lg[:], lg[:], rt[:, 2:3], None, ALU.mult).then_inc(r_dve, 1)
                        after_apart(dve, r_dve, done + 2, passed)
                        nc.vector.max(top8[:], lg[:]).then_inc(r_dve, 1)
                        after(dve, p_out, 16 * (g - 1))
                        after(dve, r_t, g - 1)
                        after_apart(dve, r_dve, done + 3, passed)
                        nc.vector.match_replace(picked[:], top8[:], lg[:], 0.0).then_inc(r_dve, 1)
                        after(dve, r_dve, done + 4)
                        nc.vector.tensor_tensor(picked[:], lg[:], picked[:], ALU.subtract).then_inc(r_dve, 1)
            run_batches(dve, step)

        @block.tensor
        def _(pe):
            mm, turn = nc.tensor.matmul, nc.tensor.transpose
            HALVES = ((0, 0), (0, 1), (1, 0))

            def turn_tiles(src, i, done):
                for c in range(2):
                    for t in range(TT):
                        last = turn(M[:, T * c + P * t:T * c + P * t + P], src[:, t, P * (2 * i + c):P * (2 * i + c) + P],
                                    ident[:])
                last.then_inc(done, 1)

            def project_T(w, act_T, i, c, done):
                for n, (hw, ha) in enumerate(HALVES):
                    for k in range(KC):
                        last = mm(A[i][:, T * c:T * c + T], w[:, hw, k, P * (2 * i + c):P * (2 * i + c) + P],
                                  act_T[:, ha, k, :], start=(n == 0 and k == 0), stop=(n == 2 and k == KC - 1))
                if c == 1:
                    last.then_inc(done, 1)

            def project(w, act_T, i, half, done):
                for k in (2 * half, 2 * half + 1):
                    for n, (ha, hw) in enumerate(HALVES):
                        last = mm(A[i][:, :], act_T[:, ha, k, P * i:P * i + P], w[:, hw, k, :],
                                  start=(k == 0 and n == 0), stop=(k == KC - 1 and n == 2))
                if half == 1:
                    last.then_inc(done, 1)

            def spread(b, jp):
                after(pe, rden_out, 2 * b + jp + 1)
                for j in range(2):
                    for q in range(TT):
                        last = turn(M[:, T * j + P * q:T * j + P * q + P],
                                    rden[:, q, 4 * j:4 * j + 4, :].rearrange("p h d -> p (h d)"), ident[:])
                last.then_inc(rden_mm, 1)

            def most(count, bound):
                return min(count, bound) if isinstance(count, int) else count

            def step(b, g, k):
                attn, prep, fin, ahead = has(b, 0, B), has(b, -1, B - 1), has(b, 1, B + 1), has(b, -2, B - 2)
                routing = has(b, GB + 1, B + 2) and k == 1
                end = isinstance(b, int)
                q = (k - 1) % GB
                for s in range(H):
                    if attn:
                        if s % 4 == 0:
                            after(pe, q_in[s // 4], 64 * (b + 1))
                            after(pe, k_in[s // 4], 64 * (b + 1))
                        after(pe, expd, H * b + s - 1)
                        for qt in range(TT):
                            last = mm(S[s % 2][:, T * qt:T * qt + T], q_stack[:, s, P * qt:P * qt + P], k_stack[:, s, :],
                                      start=True, stop=True)
                        last.then_inc(score, 1)
                    if attn if s >= 2 else fin:
                        bb, hh = (b if s >= 2 else b - 1), (s - 2) % H
                        after(pe, expd, H * bb + hh + 1)
                        after(pe, pT_dve if hh % 2 else pT_act, 8 * bb + hh // 2)
                        for kt in range(TT):
                            for qt in range(TT):
                                last = turn(TP[hh % 2][:, T * kt + P * qt:T * kt + P * qt + P],
                                            pr[:, hh % 2, qt, P * kt:P * kt + P], ident[:])
                        last.then_inc(turned, 1)
                    if s % 4 == 2 and (attn if s >= 6 else fin):
                        bb, j = (b, s // 4 - 1) if s >= 6 else (b - 1, 3)
                        after(pe, pT_act, 8 * bb + 2 * j + 2)
                        after(pe, pT_dve, 8 * bb + 2 * j + 2)
                        after(pe, v_out, 2 * (bb + 1))
                        after(pe, o_norm, 2 * bb + j // 2)
                        vp = (k if s >= 6 else k - 1) % 2
                        for kt in range(TT):
                            for c in range(4):
                                last = mm(O[32 * c:32 * c + 32, T * (j % 2):T * (j % 2) + T],
                                          v[:, vp, kt, DK * (4 * j + c):DK * (4 * j + c) + DK], pT[:, c, kt, :],
                                          start=(kt == 0), stop=(kt == TT - 1), skip_group_check=True)
                        last.then_inc(pv, 1)

                    if s == 1 and fin:
                        after(pe, lg_out, b - 1)
                        if end:
                            after(pe, xT_lo, most(2 * (b + 2), 2 * B))
                        spread(b - 1, 1)
                    if s == 2 and prep:
                        after(pe, c_in, 16 * (b + 2))
                        after(pe, o_scale, 2 * b)
                        if end:
                            after(pe, xT_lo, most(2 * (b + 2), 2 * B))
                        turn_tiles(ct, 0, cT_mm)
                    if s == 3 and routing:
                        after(pe, cT_lo, most(2 * (b + 1) + 1, 2 * B))
                        if end:
                            after(pe, lg_out, b - 1)
                            after(pe, o_scale, most(2 * b, 2 * B))
                        after(pe, r_dve, N_RDVE * g)
                        for t in range(TT):
                            last = turn(M[:, P * t:P * t + P], picked[:, P * t:P * t + P], ident[:])
                        last.then_inc(r_t, 1)
                    if s == 4 and routing:
                        after(pe, r_tout, g)
                        for t in range(TT):
                            for kk in range(GB):
                                last = mm(M[E * kk:E * kk + E, :], pickedT[:, t, E * kk:E * kk + E], x2[:, kk, t, :],
                                          start=(t == 0), stop=(t == TT - 1), skip_group_check=True)
                        last.then_inc(r_m, 1)
                    if s == 5 and routing:
                        after(pe, r_mout, g)
                        for c in range(KC):
                            last = turn(M[:, P * c:P * c + P], merged[:, P * c:P * c + P], ident[:])
                        last.then_inc(r_mt, 1)
                    if s == 6 and prep:
                        after(pe, cT_lo, 2 * (b + 1) + 1)
                        if k == 1:
                            after(pe, r_mtout, g)
                        turn_tiles(ct, 1, cT_mm)
                    if s == 9 and attn:
                        after(pe, cT_lo, most(2 * (b + 2), 2 * B))
                        if end:
                            after(pe, o_scale, 2 * b)
                        spread(b, 0)
                    if s == 10 and ahead:
                        after(pe, n1_out, 2 * (b + 3))
                        after(pe, o_scale, 2 * b + 1)
                        if end:
                            after(pe, cT_lo, 2 * (b + 2))
                        turn_tiles(xt, 0, xT_mm)
                    if s == 12 and ahead:
                        after(pe, xT_lo, 2 * (b + 2) + 1)
                        turn_tiles(xt, 1, xT_mm)
                    if s == 13 and fin:
                        after(pe, n2_out, 2 * b)
                        after(pe, xT_lo, most(2 * (b + 3), 2 * B))
                        if end:
                            after(pe, o_scale, most(2 * b + 1, 2 * B))
                        turn_tiles(x2[:, q, :, :], 0, x2T_mm)
                    if s == 14 and fin:
                        after(pe, x2T_out, 2 * (b - 1) + 1)
                        turn_tiles(x2[:, q, :, :], 1, x2T_mm)
                    if s == 15 and fin:
                        after(pe, x2T_out, 2 * b)
                        for c in range(KC):
                            last = mm(M[E * q:E * q + E, 0:T], gwT[:, c, :], x2T[:, c, :], start=(c == 0),
                                      stop=(c == KC - 1))
                        last.then_inc(lg_mm, 1)

                    i, half = s // 2 % 2, s % 2
                    if s < 4 and prep:
                        if half == 0:
                            after(pe, v_out, 2 * b + i + 1)
                            after(pe, xT_lo, 2 * (b + 2))
                        project_T(w_q, xT, i, half, q_mm)
                    if 4 <= s < 8 and fin:
                        if half == 0:
                            if prep:
                                after(pe, q_lo, 2 * (b + 1) + i + 1)
                            else:
                                after(pe, v_out, 2 * B)
                                after(pe, x2_sum, 2 * (b - 1))
                        after(pe, o_lo, 2 * (b - 1) + half + 1)
                        project(w_o, oT, i, half, o_mm)
                    if 8 <= s < 12 and prep:
                        if half == 0:
                            after(pe, x2_sum, 2 * (b - 1) + i + 1)
                            if end:
                                after(pe, q_lo, 2 * (b + 1) + i + 1)
                            after(pe, cT_lo, 2 * (b + 2))
                        project_T(w_k, cT, i, half, k_mm)
                    if s >= 12 and prep:
                        if half == 0:
                            after(pe, k_lo, 2 * (b + 1) + i + 1)
                        project(w_v, cT, i, half, v_mm)
            run_batches(pe, step)


SLOTS = 16
PER = KC + HID // D
HC = HID // D


def experts(nc, w1, w2, merged_dram, outs_dram):
    st = ExitStack()
    with st:
        sb = lambda name, shape, dt=F32: st.enter_context(nc.sbuf_tensor(name, shape, dt))
        ps = lambda name: st.enter_context(nc.psum_tensor(name, [P, 512], F32))
        sem = lambda name: st.enter_context(nc.semaphore(name))
        ring = sb("ring", [P, SLOTS, HID])
        m_raw = sb("m_raw", [P, NG, KC, GB, E])
        m = sb("m", [P, 2, KC, B])
        w1b = sb("w1b", [1, 2, HID])
        w2b = sb("w2b", [1, 2, D])
        h = sb("h", [P, 2, D])
        hT = sb("hT", [P, 2, KC, P])
        part = sb("part", [P, 2, D])
        o = sb("o", [B, 2, D])
        ident = sb("ident2", [P, P])
        fold = sb("fold", [P, B])
        ones = sb("ones2", [1, B])
        HP = [ps("HP0"), ps("HP1")]
        TPh = [ps("TPh0"), ps("TPh1")]
        OP = [ps("OP0"), ps("OP1")]
        FP = [ps("FP0"), ps("FP1")]
        piece_in = [sem(f"piece_in{i}") for i in range(SLOTS)]
        bias_in = [sem("bias_in0"), sem("bias_in1")]
        m_in, m_out, const, h_mm, h_out, t_mm, t_out, o_mm, o_out, f_mm, f_out = (
            sem(n) for n in ("fm_in", "fm_out", "fconst", "h_mm", "h_out", "t_mm", "t_out", "fo_mm", "fo_out", "f_mm", "f_out"))
        stored = [sem("stored0"), sem("stored1")]
        block = st.enter_context(nc.Block())
        NP = E // 2

        @block.sync
        def _(sp):
            sp.dma_start(m_raw[:].rearrange("p g c k e -> p g (c k e)"), merged_dram.rearrange("g p c n -> p g (c n)")).then_inc(m_in, 16)

            def expert(e, n, first):
                for i in range(PER):
                    if not first:
                        after(sp, h_mm if i < KC else o_mm, e - 1)
                    slot = PER * n + i
                    if i < KC:
                        src = w1[e, P * i:P * i + P, :]
                    else:
                        c = i - KC
                        src = w2[e, D * c:D * c + D, :].rearrange("(p s) n -> p (s n)", p=P)
                    sp.dma_start(ring[:, slot, :], src).then_inc(piece_in[slot], 16)
            expert(0, 0, True)
            expert(1, 1, True)
            with sp.Fori(1, NP) as i:
                expert(i * 2, 0, False)
                expert(i * 2 + 1, 1, False)

        @block.gpsimd
        def _(pool):
            pool.memset(ident[:], 0.0).then_inc(const, 1)
            pool.memset(ones[:], 1.0).then_inc(const, 1)
            pool.wait_ge(const, 2)
            pool.affine_select(out=ident[:], in_=ident[:], compare_op=ALU.not_equal, fill=1.0, base=0,
                               pattern=[[-1, P]], channel_multiplier=1).then_inc(const, 1)
            pool.memset(fold[:], 0.0).then_inc(const, 1)
            pool.wait_ge(const, 4)
            for c in range(HC):
                pool.affine_select(out=fold[:], in_=fold[:], compare_op=ALU.not_equal, fill=1.0, base=-B * c,
                                   pattern=[[-1, B]], channel_multiplier=1).then_inc(const, 1)
                pool.wait_ge(const, 5 + c)

            def biases(e, n, first):
                if not first:
                    after(pool, o_mm, e - 1)
                pool.dma_start(w1b[:, n, :], w1[e, D:D + 1, :]).then_inc(bias_in[n], 16)
                pool.dma_start(w2b[:, n, :], w2[e, HID:HID + 1, :]).then_inc(bias_in[n], 16)

            def store(e, n):
                after(pool, f_out, e + 1)
                pool.dma_start(outs_dram[e], o[:, n, :]).then_inc(stored[n], 16)
            biases(0, 0, True)
            biases(1, 1, True)
            with pool.Fori(1, NP) as i:
                for n in range(2):
                    store(i * 2 + n - 2, n)
                    biases(i * 2 + n, n, False)
            store(E - 2, 0)
            store(E - 1, 1)
            for n in range(2):
                pool.wait_ge(stored[n], 16 * NP)

        @block.scalar
        def _(act):
            def expert(e, n, i):
                after(act, h_mm, e + 1)
                after(act, t_mm, e - 1)
                nc.scalar.activation(h[:, n, :], HP[n][:, :], ACT.Gelu).then_inc(h_out, 1)
                after(act, f_mm, e + 1)
                after(act, stored[n], i * 16)
                nc.scalar.activation(o[:, n, :], FP[n][0:B, :], ACT.Copy).then_inc(f_out, 1)
            expert(0, 0, 0)
            expert(1, 1, 0)
            with act.Fori(1, NP) as i:
                expert(i * 2, 0, i)
                expert(i * 2 + 1, 1, i)

        @block.vector
        def _(dve):
            dve.wait_ge(m_in, 16)

            def expert(e, n):
                after(dve, h_mm, e - 1)
                nc.vector.tensor_copy(m[:, n, :, :].rearrange("p c (k g) -> p c k g", k=GB),
                                      m_raw[:, :, :, :, e].rearrange("p g c k -> p c k g")).then_inc(m_out, 1)
                after(dve, t_mm, e + 1)
                after(dve, o_mm, e - 1)
                nc.vector.tensor_copy(hT[:, n, :, :].rearrange("p s m -> p (s m)"), TPh[n][:, :]).then_inc(t_out, 1)
                after(dve, o_mm, e + 1)
                after(dve, f_mm, e - 1)
                nc.vector.tensor_copy(part[:, n, :], OP[n][:, :]).then_inc(o_out, 1)
            expert(0, 0)
            expert(1, 1)
            with dve.Fori(1, NP) as i:
                expert(i * 2, 0)
                expert(i * 2 + 1, 1)

        @block.tensor
        def _(pe):
            mm, turn = nc.tensor.matmul, nc.tensor.transpose
            pe.wait_ge(const, 4 + HC)

            def expert(e, n, i):
                after(pe, m_out, e + 1)
                after(pe, h_out, e - 1)
                after(pe, bias_in[n], 32 * i + 32)
                for k in range(KC):
                    after(pe, piece_in[PER * n + k], 16 * i + 16)
                    for c in range(HC):
                        last = mm(HP[n][B * c:B * c + B, :], m[:, n, k, :], ring[:, PER * n + k, D * c:D * c + D],
                                  start=(k == 0), stop=False, skip_group_check=True)
                for c in range(HC):
                    last = mm(HP[n][B * c:B * c + B, :], ones[:], w1b[:, n, D * c:D * c + D], start=False, stop=True,
                              skip_group_check=True)
                last.then_inc(h_mm, 1)
                after(pe, h_out, e + 1)
                after(pe, t_out, e - 1)
                for s in range(KC):
                    last = turn(TPh[n][:, P * s:P * s + P], h[:, n, s:D:KC], ident[:])
                last.then_inc(t_mm, 1)
                after(pe, t_out, e + 1)
                after(pe, o_out, e - 1)
                for c in range(HC):
                    after(pe, piece_in[PER * n + KC + c], 16 * i + 16)
                for s in range(KC):
                    for c in range(HC):
                        last = mm(OP[n][B * c:B * c + B, :], hT[:, n, s, B * c:B * c + B],
                                  ring[:, PER * n + KC + c, D * s:D * s + D], start=(s == 0), stop=(s == KC - 1 and c > 0),
                                  skip_group_check=True)
                last = mm(OP[n][0:B, :], ones[:], w2b[:, n, :], start=False, stop=True, skip_group_check=True)
                last.then_inc(o_mm, 1)
                after(pe, o_out, e + 1)
                after(pe, f_out, e - 1)
                mm(FP[n][0:B, :], fold[:], part[:, n, :], start=True, stop=True).then_inc(f_mm, 1)

            expert(0, 0, 0)
            expert(1, 1, 0)
            with pe.Fori(1, NP) as i:
                expert(i * 2, 0, i)
                expert(i * 2 + 1, 1, i)


def combine(nc, g_ffn, out, picked_dram, outs_dram):
    st = ExitStack()
    with st:
        sb = lambda name, shape, dt=F32: st.enter_context(nc.sbuf_tensor(name, shape, dt))
        sem = lambda name: st.enter_context(nc.semaphore(name))
        o = sb("o_all", [P, NG, D])
        xr = sb("xr", [P, 2, GB, TT, D])
        pz = sb("pz", [P, 2, GB, T])
        gate = sb("gate_f", [P, 2])
        Y = [st.enter_context(nc.psum_tensor(f"Y{i}", [P, D], F32)) for i in range(8)]
        N = 2 * GB
        x_in = [sem(f"x_in_f{i}") for i in range(N)]
        p_in = [sem(f"p_in_f{i}") for i in range(N)]
        x_out = [sem(f"x_out_f{i}") for i in range(N)]
        o_in, g_in, gated, zeroed, y_mm, y_sum = (sem(n) for n in ("o_in_f", "g_in_f", "gated", "zeroed", "y_mm", "y_sum"))
        block = st.enter_context(nc.Block())

        def turns(eng, turn):
            turn(0)
            with eng.Fori(1, B // N) as i:
                turn(i)

        @block.sync
        def _(sp):
            sp.dma_start(gate[:, 0:1], g_ffn.rearrange("(a n) -> a n", a=1).broadcast_to([P, 1])).then_inc(g_in, 16)
            for k in range(GB):
                sp.dma_start(o[E * k:E * k + E, :, :], outs_dram[:, NG * k:NG * k + NG, :]).then_inc(o_in, 16)
            sp.wait_ge(zeroed, 1)

            def turn(i):
                for n in range(N):
                    k = n % GB
                    after(sp, y_mm, i * 2 * N + 2 * (n + 1) - 2 * N)
                    sp.dma_start(pz[E * k:E * k + E, n // GB, k, :],
                                 picked_dram[i * 2 + n // GB, E * k:E * k + E, :]).then_inc(p_in[n], 16)
                    after(sp, x_out[n], i * 16)
                    sp.dma_start(xr[:, n // GB, k, :, :], out[i * N + n].rearrange("(t p) n -> p t n", p=P)).then_inc(x_in[n], 16)
            turns(sp, turn)

        @block.scalar
        def _(act):
            act.wait_ge(g_in, 16)
            act.activation(gate[:, 1:2], gate[:, 0:1], ACT.Tanh).then_inc(gated, 1)

            def turn(i):
                for n in range(N):
                    after(act, y_sum, i * 2 * N + 2 * (n + 1))
                    act.dma_start(out[i * N + n].rearrange("(t p) n -> p t n", p=P), xr[:, n // GB, n % GB, :, :]).then_inc(x_out[n], 16)
            turns(act, turn)
            for n in range(N):
                act.wait_ge(x_out[n], 16 * (B // N))

        @block.vector
        def _(dve):
            dve.memset(pz[:], 0.0).then_inc(zeroed, 1)
            dve.wait_ge(gated, 1)

            def turn(i):
                for n in range(N):
                    after(dve, x_in[n], i * 16 + 16)
                    for t in range(TT):
                        after(dve, y_mm, i * 2 * N + 2 * n + t + 1)
                        x_t = xr[:, n // GB, n % GB, t, :]
                        nc.vector.scalar_tensor_tensor(x_t, Y[(2 * n + t) % 8][:, :], gate[:, 1:2], x_t, ALU.mult,
                                                       ALU.add).then_inc(y_sum, 1)
            turns(dve, turn)

        @block.tensor
        def _(pe):
            pe.wait_ge(o_in, 16 * GB)

            def turn(i):
                for n in range(N):
                    after(pe, p_in[n], i * 16 + 16)
                    for t in range(TT):
                        after(pe, y_sum, i * 2 * N + 2 * n + t + 1 - 8)
                        nc.tensor.matmul(Y[(2 * n + t) % 8][:, :], pz[:, n // GB, n % GB, P * t:P * t + P],
                                         o[:, i * 2 + n // GB, :], start=True, stop=True).then_inc(y_mm, 1)
            turns(pe, turn)


def build(nc, A, out):
    merged_dram = nc.dram_tensor("merged_scratch", [NG, P, KC, P], F32, kind="Internal").ap()
    picked_dram = nc.dram_tensor("picked_scratch", [NG, P, T], F32, kind="Internal").ap()
    outs_dram = nc.dram_tensor("outs_scratch", [E, B, D], F32, kind="Internal").ap()
    attention_and_routing(nc, A["x"], A["ctx_1024"], A["g_xattn"], A["L0_xattn_Wq"], A["L0_xattn_bq"], A["L0_xattn_Wk"],
                          A["L0_xattn_bk"], A["L0_xattn_Wv"], A["L0_xattn_bv"], A["L0_xattn_Wo"], A["L0_xattn_bo"],
                          A["L0_ffn_gate_w"], A["L0_ffn_gate_b"], out, merged_dram, picked_dram)
    experts(nc, A["L0_ffn_w1"], A["L0_ffn_w2"], merged_dram, outs_dram)
    combine(nc, A["g_ffn"], out, picked_dram, outs_dram)


def kernel(**inputs):
    import concourse.bacc as bacc
    from concourse.bass_utils import run_bass_kernel_spmd

    nc = bacc.Bacc("TRN2", target_bir_lowering=False, num_devices=1)
    arrays, aps = {}, {}
    for name, a in inputs.items():
        a = np.ascontiguousarray(a)
        arrays[name + "_in"] = a
        aps[name] = nc.dram_tensor(name + "_in", a.shape, mybir.dt.from_np(a.dtype), kind="ExternalInput").ap()
    out = nc.dram_tensor("y_out", [B, T, D], F32, kind="ExternalOutput").ap()
    build(nc, aps, out)
    return run_bass_kernel_spmd(nc, [arrays], core_ids=[0]).results[0]["y_out"]
```

```python
from contextlib import ExitStack

import numpy as np

import concourse.bass as bass
from concourse import mybir
from concourse.alu_op_type import AluOpType as ALU

F32 = mybir.dt.float32
F32R = mybir.dt.float32r
ACT = mybir.ActivationFunctionType
AX = mybir.AxisListType

B, T, D = 32, 256, 512
H, DK = 16, 32
E, HID, TOP = 32, 2048, 8
P = 128
KC = D // P
TT = T // P
GB = 4
NG = B // GB
HB = H // 4
SCALE = float(DK) ** -0.5
EPS = 1e-5


def after(eng, sem, count):
    if isinstance(count, int) and count <= 0:
        return
    eng.wait_ge(sem, count)


def after_apart(eng, sem, count, passed):
    if isinstance(count, int) and count <= 0:
        return
    eng.wait_ge(sem, count)
    eng.sem_inc(passed, 1)


def run_batches(eng, step):
    for b in range(-2, 2 * GB):
        step(b, b // GB, b % GB)
    with eng.Fori(2, NG - 1) as g:
        for k in range(GB):
            step(g * GB + k, g, k)
    for b in range(B - GB, B + 2):
        step(b, b // GB, b % GB)


def has(b, low, high):
    return low <= b < high if isinstance(b, int) else True


SLOTS = 16
PER = KC + HID // D
HC = HID // D
EARLY = 14


class Shared:

    def __init__(self, nc, st):
        sb = lambda name, shape, dt=F32: st.enter_context(nc.sbuf_tensor(name, shape, dt))
        sem = lambda name: st.enter_context(nc.semaphore(name))
        self.ring = sb("ring", [P, SLOTS, HID])
        self.m_raw = sb("m_raw", [P, NG, KC, GB, E])
        self.w1b = sb("w1b", [1, 2, HID])
        self.w2b = sb("w2b", [1, 2, D])
        self.start = nc.sbuf_base - 4 * (SLOTS * HID + NG * KC * P + 2 * HID + 2 * D)
        self.nc = nc
        self.ident = sb("ident", [P, P])
        self.fold = sb("fold", [P, B])
        self.ones = sb("ones", [1, P])
        self.piece_in = [sem(f"piece_in{i}") for i in range(SLOTS)]
        self.m_in = sem("m_in_raw")
        self.bias_in = [sem("bias_in0"), sem("bias_in1")]

    def over(self, name, word, shape, dt=F32):
        return self.nc.alloc_sbuf_tensor_at(name, shape, dt, offset=self.start + 4 * word)

    def load_biases(self, eng, w1, w2, e, n):
        eng.dma_start(self.w1b[:, n, :], w1[e, D:D + 1, :]).then_inc(self.bias_in[n], 16)
        eng.dma_start(self.w2b[:, n, :], w2[e, HID:HID + 1, :]).then_inc(self.bias_in[n], 16)

    def load_piece(self, sp, w1, w2, e, n, i):
        slot = PER * n + i
        if i < KC:
            src = w1[e, P * i:P * i + P, :]
        else:
            c = i - KC
            src = w2[e, D * c:D * c + D, :].rearrange("(p s) n -> p (s n)", p=P)
        sp.dma_start(self.ring[:, slot, :], src).then_inc(self.piece_in[slot], 16)


class Joint:

    def __init__(self, nc, st, sh):
        sem = lambda name: st.enter_context(nc.semaphore(name))
        self.outs = st.enter_context(nc.sbuf_tensor("outs", [P, NG, D], F32))
        self.xr = sh.over("xr", 0, [P, 2, GB, TT, D])
        self.pz = sh.over("pz", 2 * GB * TT * D, [P, 2, GB, T])
        self.gate = st.enter_context(nc.sbuf_tensor("gate_f", [P, 2], F32))
        self.x_in = [sem(f"x_in_f{i}") for i in range(2 * GB)]
        self.p_in = [sem(f"p_in_f{i}") for i in range(2 * GB)]
        self.g_in, self.zeroed = sem("g_in_f"), sem("zeroed")
        self.outs_in = sem("outs_in")

    def load_x(self, sp, out, i, n):
        sp.dma_start(self.xr[:, n // GB, n % GB, :, :],
                     out[i * 2 * GB + n].rearrange("(t p) n -> p t n", p=P)).then_inc(self.x_in[n], 16)

    def load_picked(self, sp, picked_dram, i, n):
        k = n % GB
        sp.dma_start(self.pz[E * k:E * k + E, n // GB, k, :],
                     picked_dram[i * 2 + n // GB, E * k:E * k + E, :]).then_inc(self.p_in[n], 16)


def attention_and_routing(nc, sh, w1, w2, x, ctx, g_xattn, wq, bq, wk, bk, wv, bv, wo, bo, gate_w, gate_b, out, merged_dram,
                          picked_dram):
    st = ExitStack()
    with st:
        sb = lambda name, shape, dt=F32: st.enter_context(nc.sbuf_tensor(name, shape, dt))
        ps = lambda name: st.enter_context(nc.psum_tensor(name, [P, 512], F32))
        sem = lambda name: st.enter_context(nc.semaphore(name))

        two = 2 * HID
        w_q, w_k, w_v, w_o = (sh.over(n, i * two, [P, 2, KC, D], F32R) for i, n in enumerate(("w_q", "w_k", "w_v", "w_o")))
        q_stack = sh.over("q_stack", 4 * two, [P, H, T], F32R)
        k_stack = sh.over("k_stack", 5 * two, [P, H, T], F32R)
        qk = sh.over("qk", 6 * two, [P, 4, HB, T])
        x2 = sh.over("x2", 7 * two, [P, GB, TT, D])
        merged_at = 8 * two
        biases_at = merged_at + NG * KC * P
        xt = sh.over("xt", merged_at, [P, TT, D])
        xT = sh.over("xT", merged_at + TT * D, [P, 2, KC, T], F32R)
        ct = sh.over("ct", biases_at, [P, TT, D])
        cT = sh.over("cT", biases_at + TT * D, [P, 2, KC, T], F32R)
        v = sh.over("v", biases_at + TT * D + 2 * KC * T, [P, 2, TT, D])
        pr = sb("pr", [P, 2, TT, T])
        pT = sb("pT", [P, 4, TT, T])
        den = sb("den", [P, 2, H // 2, TT])
        rden = sb("rden", [P, TT, H // 2, DK])
        rs = sb("rs", [P, H // 2, TT])
        negmax = sb("negmax", [P, 2, TT])
        o_n = sb("o_n", [P, 2, 2, T])
        oT = sb("oT", [P, 2, KC, T], F32R)
        x2T = sb("x2T", [P, KC, T])
        lg = sb("lg", [P, T])
        picked = sb("picked", [P, T])
        pickedT = sb("pickedT", [P, TT, P])
        merged = sb("merged", [P, D])
        mergedT = sh.m_raw[:, NG - 1, :, :, :].rearrange("p k a e -> p k (a e)")
        top8 = sb("top8", [P, TOP])
        rt = sb("rt", [P, 4])
        ln1 = sb("ln1", [P, 32])
        ln2 = sb("ln2", [P, 32])
        ident, ones, fold = sh.ident, sh.ones, sh.fold
        bv_col = sb("bv_col", [P, KC])
        res_bias = sb("res_bias", [P, D])
        bqk = sb("bqk", [P, 3, HB])
        gwT = sb("gwT", [P, KC, E])
        gb = sb("gb", [P, 1])
        gate = sb("gate", [P, 2])
        eps = sb("eps", [P, 1])

        S = [ps("S0"), ps("S1")]
        TP = [ps("TP0"), ps("TP1")]
        A = [ps("A0"), ps("A1")]
        O = ps("O")
        M = ps("M")

        x_in = sem("x_in")
        load = [sem(f"load_{n}") for n in ("wq", "wk", "wv", "wo")]
        bv_in, g_in, bqk_in, gw_in, const, split_hi, split_lo, setup_mm, setup_v, setup_a = (
            sem(n) for n in ("bv_in", "g_in", "bqk_in", "gw_in", "const", "split_hi", "split_lo", "setup_mm", "setup_v", "setup_a"))
        bv_wide, bo_row, gw = pT[:, 0:2, :, :].rearrange("p a c t -> p (a c t)")[:, 0:KC * P], pT[0:1, 2, :, :], pT[0:E, 3, :, :]
        bv_wide = bv_wide.rearrange("p (k m) -> p k m", k=KC)
        bo_row, gw = (a.rearrange("p c t -> p (c t)") for a in (bo_row, gw))
        raw = [qk[:, 2 * i:2 * i + 2, :, :].rearrange("p a c t -> p (a c t)").rearrange("p (k n) -> p k n", k=KC)
               for i in range(2)]
        raw += [x2[:, 2 * i:2 * i + 2, :, :].rearrange("p a c t -> p (a c t)").rearrange("p (k n) -> p k n", k=KC)
                for i in range(2)]
        weights = [w_q, w_k, w_v, w_o]

        def pieces(i, k):
            if i >= 2:
                return [(raw[i][:, k, :], [weights[i][:, half, k, :] for half in range(2)])]
            src = raw[i][:, k, :].rearrange("p (j c d) -> p c j d", j=4, c=4)
            return [(src[:, c], [weights[i][:, half, k, P * c:P * c + P].rearrange("p (j d) -> p j d", j=4)
                                 for half in range(2)]) for c in range(4)]

        ORDER = (3, 0, 1, 2)
        with nc.Block() as block:

            @block.sync
            def _(sp):
                sp.dma_start(bv_col[:], bv.rearrange("(k p) -> p k", p=P),
                             allow_slow_non_contiguous=True).then_inc(bv_in, 16)
                sp.dma_start(bo_row, bo.rearrange("(a n) -> a n", a=1)).then_inc(bv_in, 16)
                sp.dma_start(gate[:, 0:1], g_xattn.rearrange("(a n) -> a n", a=1).broadcast_to([P, 1])).then_inc(g_in, 16)
                for i in ORDER:
                    w = (wq, wk, wv, wo)[i]
                    sp.dma_start(raw[i], w.rearrange("(k p) n -> p k n", p=P)).then_inc(load[i], 16)
                sp.dma_start(gw, gate_w).then_inc(gw_in, 16)
                for j in range(GB):
                    sp.dma_start(gb[E * j:E * j + E, :], gate_b.rearrange("(e a) -> e a", a=1)).then_inc(gw_in, 16)
                sp.wait_ge(gw_in, 16 * (1 + GB))
                sp.dma_start(xt[:], x[0].rearrange("(t p) n -> p t n", p=P)).then_inc(x_in, 16)

            @block.gpsimd
            def _(pool):
                pool.memset(ident[:], 0.0).then_inc(const, 1)
                pool.wait_ge(const, 1)
                pool.affine_select(out=ident[:], in_=ident[:], compare_op=ALU.not_equal, fill=1.0, base=0,
                                   pattern=[[-1, P]], channel_multiplier=1).then_inc(const, 1)
                pool.memset(ones[:], 1.0).then_inc(const, 1)
                pool.memset(eps[:], EPS).then_inc(const, 1)
                for i, bias in enumerate((bq, bk)):
                    for j in range(4):
                        pool.dma_start(bqk[32 * j:32 * j + 32, i, :],
                                       bias[P * j:P * j + P].rearrange("(c d) -> d c", d=DK),
                                       allow_slow_non_contiguous=True).then_inc(bqk_in, 16)
                pool.memset(fold[:], 0.0).then_inc(const, 1)
                pool.wait_ge(const, 5)
                for c in range(HC):
                    pool.affine_select(out=fold[:], in_=fold[:], compare_op=ALU.not_equal, fill=1.0, base=-B * c,
                                       pattern=[[-1, B]], channel_multiplier=1).then_inc(const, 1)
                    pool.wait_ge(const, 6 + c)

            @block.scalar
            def _(act):
                act.wait_ge(g_in, 16)
                act.activation(gate[:, 1:2], gate[:, 0:1], ACT.Tanh).then_inc(setup_a, 1)
                for i in ORDER:
                    act.wait_ge(load[i], 16)
                    for k in range(KC):
                        for src, dst in pieces(i, k):
                            last = act.activation(dst[0], src, ACT.Copy, scale=SCALE if i == 0 else 1.0)
                        last.then_inc(split_hi, 1)
                act.wait_ge(setup_a, 1)
                act.wait_ge(setup_mm, 1)
                act.activation(res_bias[:], A[0][:, :], ACT.Copy, scale=gate[:, 1:2]).then_inc(setup_a, 1)
                act.wait_ge(setup_mm, 2)
                act.activation(gwT[:].rearrange("p k e -> p (k e)"), A[1][:, 0:KC * E], ACT.Copy).then_inc(setup_a, 1)

            @block.vector
            def _(dve):
                dve.wait_ge(bv_in, 32)
                for k in range(KC):
                    dve.tensor_copy(bv_wide[:, k, :], bv_col[:, k:k + 1].broadcast_to([P, P])).then_inc(setup_v, 1)
                for n, i in enumerate(ORDER):
                    dve.wait_ge(load[i], 16)
                    for k in range(KC):
                        dve.wait_ge(split_hi, KC * n + k + 1)
                        for src, dst in pieces(i, k):
                            last = dve.scalar_tensor_tensor(dst[1], src, SCALE if i == 0 else 1.0, dst[0], ALU.mult,
                                                            ALU.subtract)
                        last.then_inc(split_lo, 1)
                dve.wait_ge(bqk_in, 16 * 8)
                dve.tensor_scalar(bqk[:, 2, :], bqk[:, 0, :], SCALE, None, ALU.mult).then_inc(setup_v, 1)

            @block.tensor
            def _(pe):
                pe.wait_ge(setup_v, KC)
                pe.wait_ge(const, 4)
                pe.wait_ge(load[3], 16)
                pe.wait_ge(bv_in, 32)
                for k in range(KC):
                    nc.tensor.matmul(A[0][:, :], bv_wide[:, k, :], raw[3][:, k, :], start=(k == 0), stop=False)
                nc.tensor.matmul(A[0][:, :], ones[:], bo_row, start=False, stop=True).then_inc(setup_mm, 1)
                pe.wait_ge(gw_in, 16 * (1 + GB))
                for k in range(KC):
                    last = nc.tensor.transpose(A[1][:, E * k:E * k + E], gw[:, P * k:P * k + P], ident[0:E, 0:E])
                last.then_inc(setup_mm, 1)

        c_in, x2_out, m_out, p_out = (sem(n) for n in ("c_in", "x2_out", "m_out", "p_out"))
        r_in = [sem(f"r_in{q}") for q in range(GB)]
        q_in = [sem(f"q_in{j}") for j in range(4)]
        k_in = [sem(f"k_in{j}") for j in range(4)]
        n1_sum, n1_mom, n1_guess, n1_step, n1_out = (sem(n) for n in ("n1_sum", "n1_mom", "n1_guess", "n1_step", "n1_out"))
        n2_sum, n2_mom, n2_guess, n2_step, n2_out = (sem(n) for n in ("n2_sum", "n2_mom", "n2_guess", "n2_step", "n2_out"))
        xT_mm, cT_mm, q_mm, k_mm, v_mm, o_mm, x2T_mm = (
            sem(n) for n in ("xT_mm", "cT_mm", "q_mm", "k_mm", "v_mm", "o_mm", "x2T_mm"))
        xT_hi, xT_lo, cT_hi, cT_lo, q_hi, q_lo, k_hi, k_lo = (
            sem(n) for n in ("xT_hi", "xT_lo", "cT_hi", "cT_lo", "q_hi", "q_lo", "k_hi", "k_lo"))
        v_out, x2_sum, x2T_out = (sem(n) for n in ("v_out", "x2_sum", "x2T_out"))
        score, maxed, expd, turned = (sem(n) for n in ("score", "maxed", "expd", "turned"))
        pT_act, pT_dve = sem("pT_act"), sem("pT_dve")
        pv = sem("pv")
        rsum, rden_out, rden_mm, o_scale, o_norm, o_hi, o_lo = (
            sem(n) for n in ("rsum", "rden_out", "rden_mm", "o_scale", "o_norm", "o_hi", "o_lo"))
        res = sem("res")
        lg_mm, lg_out = sem("lg_mm"), sem("lg_out")
        r_max, r_exp, r_dve, r_t, r_tout, r_m, r_mout, r_mt, r_mtout = (
            sem(n) for n in ("r_max", "r_exp", "r_dve", "r_t", "r_tout", "r_m", "r_mout", "r_mt", "r_mtout"))
        N_RDVE = 5
        passed, passed_pool = sem("passed"), sem("passed_pool")

        block = st.enter_context(nc.Block())


        @block.sync
        def _(sp):
            def fill_stack(j, stack, first, parts, done):
                for r in range(4):
                    sp.dma_start(stack[32 * r:32 * r + 32, 4 * j:4 * j + 4, :].bitcast(F32),
                                 qk[32 * j:32 * j + 32, first + parts[r], :, :]).then_inc(done, 16)

            def load(dst, src, done):
                sp.dma_start(dst[:], src.rearrange("(t p) n -> p t n", p=P)).then_inc(done, 16)

            def step(b, g, k):
                prep = has(b, -1, B - 1)
                if prep:
                    after(sp, q_lo, 2 * (b + 2))
                    for j in range(2):
                        after(sp, score, H * b + 4 * j + 4)
                        fill_stack(j, q_stack, 0, (0, 1, 0, 1), q_in[j])
                if has(b, -2, B - 2):
                    after(sp, cT_mm, 2 * (b + 2))
                    load(ct, ctx[b + 2], c_in)
                if prep:
                    after(sp, score, H * b + 12)
                    fill_stack(2, q_stack, 0, (0, 1, 0, 1), q_in[2])
                if has(b, -2, B - 3):
                    after(sp, xT_mm, 2 * (b + 3))
                    load(xt, x[b + 3], x_in)
                if prep:
                    after(sp, k_lo, 2 * (b + 2))
                    for j in range(3):
                        fill_stack(j, k_stack, 2, (0, 0, 1, 1), k_in[j])
                    after(sp, score, H * b + H)
                    fill_stack(3, q_stack, 0, (0, 1, 0, 1), q_in[3])
                    fill_stack(3, k_stack, 2, (0, 0, 1, 1), k_in[3])
            run_batches(sp, step)
            def pieces_to(*ring_slots):
                for slot in ring_slots:
                    sh.load_piece(sp, w1, w2, slot // PER, slot // PER, slot % PER)
            sp.wait_ge(v_mm, 2 * B)
            pieces_to(0, 1, 2)
            sp.wait_ge(x2_out, 16 * (B - 1))
            sp.wait_ge(r_in[GB - 1], 16 * NG)
            pieces_to(3, 4)
            sp.wait_ge(score, H * B)
            pieces_to(8, 9, 10)
            sp.wait_ge(x2_out, 16 * B)
            sp.wait_ge(q_mm, 2 * B)
            sp.wait_ge(m_out, 16 * (NG - 1))
            sp.dma_start(sh.m_raw[:, 0:NG - 1, :, :, :].rearrange("p g c k e -> p g (c k e)"),
                         merged_dram.rearrange("g p c n -> p g (c n)")).then_inc(sh.m_in, 16)
            sp.wait_ge(o_mm, 2 * B)
            pieces_to(5, 6)
            sp.wait_ge(p_out, 16 * NG)
            pieces_to(7, 11, 12, 13)

        @block.gpsimd
        def _(pool):
            def load_again(n, q, merged_groups):
                after_apart(pool, r_m, merged_groups, passed_pool)
                pool.dma_start(x2[:, q, :, :], x[n].rearrange("(t p) n -> p t n", p=P)).then_inc(r_in[q], 16)

            def step(b, g, k):
                routing = has(b, GB + 1, B + 2) and k == 1
                if routing:
                    after_apart(pool, r_dve, N_RDVE * g, passed_pool)
                    pool.dma_start(picked_dram[g - 1], picked[:]).then_inc(p_out, 16)
                if has(b, 1, B + 1):
                    q = (k - 1) % GB
                    if k == 1:
                        load_again(b - 1, q, g)
                    after(pool, r_in[q], 16 * (g if k == 0 else g + 1))
                    for t in range(TT):
                        last = nc.gpsimd.tensor_tensor(x2[:, q, t, :], x2[:, q, t, :], res_bias[:], ALU.add)
                    last.then_inc(res, 1)
                    after_apart(pool, x2_sum, 2 * b, passed_pool)
                    pool.dma_start(out[b - 1].rearrange("(t p) n -> p t n", p=P), x2[:, q, :, :]).then_inc(x2_out, 16)
                if has(b, 1, B) and k != 0:
                    load_again(b, k, g)
                if routing and has(b, 0, B):
                    after_apart(pool, r_mtout, g, passed_pool)
                    pool.dma_start(merged_dram[g - 1], mergedT[:]).then_inc(m_out, 16)
            run_batches(pool, step)
            pool.wait_ge(pv, 4 * B)
            for n in range(2):
                sh.load_biases(pool, w1, w2, n, n)
            pool.wait_ge(x2_out, 16 * B)
            pool.wait_ge(m_out, 16 * (NG - 1))
            pool.wait_ge(p_out, 16 * NG)

        @block.scalar
        def _(act):
            act.preload_act_table_set("natural_log_exp_and_others")

            def copy(dst, src):
                return nc.scalar.activation(dst, src, ACT.Copy)

            def norm_guess(n, mom, guess, tile):
                after(act, mom, 2 * n + 2)
                nc.scalar.activation(tile[:, 20:22], tile[:, 13:16:2], ACT.Ln, bias=eps[:]).then_inc(guess, 1)
                after(act, guess, 2 * n + 1)
                nc.scalar.activation(tile[:, 22:24], tile[:, 20:22], ACT.Exp, scale=-0.5).then_inc(guess, 1)

            def exps(b, s):
                t = H * b + s
                after(act, maxed, t + 1)
                after(act, turned, t - 1)
                if s % 8 == 0:
                    after(act, rsum, 2 * b + s // 8 - 1)
                for q in range(TT):
                    last = nc.scalar.activation(pr[:, s % 2, q, :], S[s % 2][:, T * q:T * q + T], ACT.Exp,
                                                bias=negmax[:, s % 2, q:q + 1],
                                                accum_out=den[:, s // 8, s % 8, q:q + 1])
                last.then_inc(expd, 1)

            def take_pT(b, s):
                after(act, turned, H * b + s + 1)
                after(act, pv, 4 * b + s // 4)
                copy(pT[:, s % 4, :, :].rearrange("p a t -> p (a t)"), TP[s % 2][:, :]).then_inc(pT_act, 1)

            def high_half_qk(b, i, kind):
                fill, done = ((q_mm, q_hi), (k_mm, k_hi))[kind]
                if i == 0:
                    for j in range(4):
                        after(act, (q_in, k_in)[kind][j], 64 * b)
                after(act, fill, 2 * b + i + 1)
                for c in range(2):
                    bias = bqk[:, 2 if kind == 0 else 1, 2 * i + c:2 * i + c + 1]
                    last = nc.scalar.activation(qk[:, 2 * kind, 2 * i + c, :].bitcast(F32R),
                                                A[i][:, T * c:T * c + T], ACT.Identity, bias=bias)
                last.then_inc(done, 1)

            def take_v(b, i, par):
                after(act, v_mm, 2 * b + i + 1)
                after(act, pv, 4 * (b - 1))
                copy(v[:, par, i, :], A[i][:, :]).then_inc(v_out, 1)

            def scale(b, jp):
                after(act, rden_mm, 2 * b + jp + 1)
                after(act, o_lo, 2 * b + jp - 1)
                copy(o_n[:, jp, :, :].rearrange("p a t -> p (a t)"), M[:, :]).then_inc(o_scale, 1)

            def high_half_o(b, jp):
                after(act, o_norm, 2 * b + jp + 1)
                after(act, o_mm, 2 * b)
                copy(oT[:, 0, 2 * jp:2 * jp + 2, :], o_n[:, jp, :, :]).then_inc(o_hi, 1)

            def step(b, g, k):
                attn, prep, fin, ahead = has(b, 0, B), has(b, -1, B - 1), has(b, 1, B + 1), has(b, -2, B - 2)
                routing = has(b, GB + 1, B + 2) and k == 1
                for s in range(H):
                    if attn:
                        exps(b, s)
                    if s % 2 == 0 and (attn if s >= 2 else fin):
                        take_pT(b if s >= 2 else b - 1, (s - 2) % H)
                    if s == 1 and fin:
                        scale(b - 1, 1)
                    if s == 3 and routing:
                        after(act, r_t, g)
                        copy(pickedT[:].rearrange("p a t -> p (a t)"), M[:, 0:TT * P]).then_inc(r_tout, 1)
                    if s == 4 and routing:
                        after(act, r_m, g)
                        copy(merged[:], M[:, :]).then_inc(r_mout, 1)
                    if s == 5 and routing:
                        after(act, r_mt, g)
                        after(act, m_out, 16 * (g - 1))
                        copy(mergedT[:].rearrange("p a t -> p (a t)"), M[:, :]).then_inc(r_mtout, 1)
                    if s == 9 and attn:
                        scale(b, 0)
                    if s in (13, 14) and fin:
                        i = s - 13
                        after(act, lg_mm, b - 1)
                        after(act, x2T_mm, 2 * (b - 1) + i + 1)
                        copy(x2T[:, 2 * i:2 * i + 2, :].rearrange("p a t -> p (a t)"), M[:, :]).then_inc(x2T_out, 1)
                    if s == 15 and fin:
                        q = (k - 1) % GB
                        after(act, lg_mm, b)
                        if q == 0:
                            after(act, r_dve, N_RDVE * g)
                        nc.scalar.activation(lg[E * q:E * q + E, :], M[E * q:E * q + E, 0:T], ACT.Identity,
                                             bias=gb[E * q:E * q + E, :]).then_inc(lg_out, 1)
                    if s == 0 and attn:
                        take_v(b, 1, k % 2)
                    if s in (2, 4) and prep:
                        high_half_qk(b + 1, (s - 2) // 2, 0)
                    if s in (10, 12) and prep:
                        high_half_qk(b + 1, (s - 10) // 2, 1)
                    if s == 14 and prep:
                        take_v(b + 1, 0, (k + 1) % 2)
                    if s == 3 and fin:
                        high_half_o(b - 1, 1)
                    if s == 12 and attn:
                        high_half_o(b, 0)
                    if s == 2 and ahead:
                        norm_guess(b + 2, n1_mom, n1_guess, ln1)
                    if s == 9 and fin:
                        norm_guess(b - 1, n2_mom, n2_guess, ln2)
                    if s == 0 and routing:
                        after(act, r_max, g)
                        nc.scalar.activation(lg[:], lg[:], ACT.Exp, bias=rt[:, 0:1], accum_out=rt[:, 1:2]).then_inc(r_exp, 1)
            run_batches(act, step)

        @block.vector
        def _(dve):
            def norm_sums(n, t, src, tile, s_sum, s_mom):
                nc.vector.bn_stats(tile[:, 6 * t:6 * t + 6], src[:, t, :]).then_inc(s_sum, 1)
                if t == TT - 1:
                    after_apart(dve, s_sum, 2 * n + 2, passed)
                    for t in range(TT):
                        nc.vector.bn_aggr(tile[:, 12 + 2 * t:14 + 2 * t], tile[:, 6 * t:6 * t + 6]).then_inc(s_mom, 1)

            def norm_step(n, tile, guess, s_step):
                var, y, a = tile[:, 13:16:2], tile[:, 22:24], tile[:, 24:26]
                after(dve, guess, 2 * n + 2)
                nc.vector.scalar_tensor_tensor(a, var, EPS, y, ALU.add, ALU.mult).then_inc(s_step, 1)
                after(dve, s_step, 4 * n + 1)
                nc.vector.tensor_tensor(tile[:, 26:28], a, y, ALU.mult).then_inc(s_step, 1)
                after(dve, s_step, 4 * n + 2)
                nc.vector.tensor_scalar(tile[:, 28:30], tile[:, 26:28], -0.5, 1.5, ALU.mult, ALU.add).then_inc(s_step, 1)
                after(dve, s_step, 4 * n + 3)
                nc.vector.tensor_tensor(tile[:, 30:32], tile[:, 28:30], y, ALU.mult).then_inc(s_step, 1)

            def norm_apply(n, src, tile, s_step, s_out):
                after(dve, s_step, 4 * n + 4)
                for t in range(TT):
                    nc.vector.tensor_scalar(src[:, t, :], src[:, t, :], tile[:, 12 + 2 * t:13 + 2 * t],
                                            tile[:, 30 + t:31 + t], ALU.subtract, ALU.mult).then_inc(s_out, 1)

            def both_halves(n, i, dst, fill, hi, lo):
                after(dve, fill, 2 * n + i + 1)
                nc.vector.tensor_copy(dst[:, 0, 2 * i:2 * i + 2, :].rearrange("p a t -> p (a t)"), M[:, :]).then_inc(hi, 1)
                after(dve, hi, 2 * n + i + 1)
                nc.vector.tensor_tensor(dst[:, 1, 2 * i:2 * i + 2, :].rearrange("p a t -> p (a t)"), M[:, :],
                                        dst[:, 0, 2 * i:2 * i + 2, :].rearrange("p a t -> p (a t)"),
                                        ALU.subtract).then_inc(lo, 1)

            def low_half_qk(b, i, kind):
                hi, lo = ((q_hi, q_lo), (k_hi, k_lo))[kind]
                after(dve, hi, 2 * b + i + 1)
                for c in range(2):
                    cc = 2 * i + c
                    bias = bqk[:, 2 if kind == 0 else 1, cc:cc + 1]
                    last = nc.vector.scalar_tensor_tensor(
                        qk[:, 2 * kind + 1, cc, :].bitcast(F32R), A[i][:, T * c:T * c + T], bias,
                        qk[:, 2 * kind, cc, :], ALU.add, ALU.subtract)
                last.then_inc(lo, 1)

            def invert(b, jp):
                after(dve, expd, H * b + 8 * jp + 8)
                nc.vector.reciprocal(rs[:], den[:, jp, :, :]).then_inc(rsum, 1)
                after(dve, rsum, 2 * b + jp + 1)
                after(dve, rden_mm, 2 * b + jp)
                nc.vector.tensor_copy(rden[:].rearrange("p q h d -> p h q d"),
                                      rs[:].unsqueeze(3).broadcast_to([P, H // 2, TT, DK])).then_inc(rden_out, 1)

            def normalise(b, jp):
                after(dve, pv, 4 * b + 2 * jp + 2)
                after(dve, o_scale, 2 * b + jp + 1)
                o = o_n[:, jp, :, :].rearrange("p a t -> p (a t)")
                nc.vector.tensor_tensor(o, O[:, :], o, ALU.mult).then_inc(o_norm, 1)

            def low_half_o(b, jp):
                after(dve, o_hi, 2 * b + jp + 1)
                nc.vector.tensor_tensor(oT[:, 1, 2 * jp:2 * jp + 2, :], o_n[:, jp, :, :],
                                        oT[:, 0, 2 * jp:2 * jp + 2, :], ALU.subtract).then_inc(o_lo, 1)

            def step(b, g, k):
                attn, prep, fin, ahead = has(b, 0, B), has(b, -1, B - 1), has(b, 1, B + 1), has(b, -2, B - 2)
                q = (k - 1) % GB
                for s in range(H):
                    if attn:
                        after(dve, score, H * b + s + 1)
                        nc.vector.reduce_max(negmax[:, s % 2, :], S[s % 2][:, :].rearrange("p (q t) -> p q t", q=TT),
                                             axis=AX.X, negate=True).then_inc(maxed, 1)
                    if s in (3, 11) and prep:
                        low_half_qk(b + 1, 0, s // 8)
                    if s == 8 and attn:
                        invert(b, 0)
                    if s % 2 == 1 and (attn if s >= 2 else fin):
                        bb, hh = (b if s >= 2 else b - 1), (s - 2) % H
                        after(dve, turned, H * bb + hh + 1)
                        after(dve, pv, 4 * bb + hh // 4)
                        nc.vector.tensor_copy(pT[:, hh % 4, :, :].rearrange("p a t -> p (a t)"),
                                              TP[hh % 2][:, :]).then_inc(pT_dve, 1)
                    if s in (5, 13) and prep:
                        low_half_qk(b + 1, 1, s // 8)
                    if s in (6, 8) and fin:
                        i = (s - 6) // 2
                        after(dve, res, b)
                        after(dve, o_mm, 2 * (b - 1) + i + 1)
                        nc.vector.scalar_tensor_tensor(x2[:, q, i, :], A[i][:, :], gate[:, 1:2], x2[:, q, i, :],
                                                       ALU.mult, ALU.add).then_inc(x2_sum, 1)
                    if s in (2, 6) and prep:
                        after(dve, v_mm, 2 * (b + 1))
                        both_halves(b + 1, (s - 2) // 4, cT, cT_mm, cT_hi, cT_lo)
                    if s in (10, 12) and ahead:
                        after(dve, q_mm, 2 * (b + 2))
                        both_halves(b + 2, (s - 10) // 2, xT, xT_mm, xT_hi, xT_lo)
                    if s == 0 and fin:
                        invert(b - 1, 1)
                    if s == 2 and fin:
                        normalise(b - 1, 1)
                    if s == 4 and fin:
                        low_half_o(b - 1, 1)
                    if s == 11 and attn:
                        normalise(b, 0)
                    if s == 14 and attn:
                        low_half_o(b, 0)
                    if s in (7, 8) and fin:
                        after(dve, x2_sum, 2 * (b - 1) + s - 6)
                        norm_sums(b - 1, s - 7, x2[:, q, :, :], ln2, n2_sum, n2_mom)
                    if s == 10 and fin:
                        norm_step(b - 1, ln2, n2_guess, n2_step)
                    if s == 12 and fin:
                        after(dve, x2_out, 16 * b)
                        norm_apply(b - 1, x2[:, q, :, :], ln2, n2_step, n2_out)
                    if s in (0, 1) and ahead:
                        after(dve, x_in, 16 * (b + 3))
                        norm_sums(b + 2, s, xt, ln1, n1_sum, n1_mom)
                    if s == 4 and ahead:
                        norm_step(b + 2, ln1, n1_guess, n1_step)
                    if s == 7 and ahead:
                        norm_apply(b + 2, xt, ln1, n1_step, n1_out)
                    if s == 0 and has(b, GB + 1, B + 2) and k == 1:
                        after(dve, lg_out, b - 1)
                        nc.vector.reduce_max(rt[:, 0:1], lg[:], axis=AX.X, negate=True).then_inc(r_max, 1)
                    if s == 1 and has(b, GB + 1, B + 2) and k == 1:
                        done = N_RDVE * (g - 1)
                        after(dve, r_exp, g)
                        nc.vector.reciprocal(rt[:, 2:3], rt[:, 1:2]).then_inc(r_dve, 1)
                        after(dve, r_dve, done + 1)
                        nc.vector.tensor_scalar(lg[:], lg[:], rt[:, 2:3], None, ALU.mult).then_inc(r_dve, 1)
                        after_apart(dve, r_dve, done + 2, passed)
                        nc.vector.max(top8[:], lg[:]).then_inc(r_dve, 1)
                        after(dve, p_out, 16 * (g - 1))
                        after(dve, r_t, g - 1)
                        after_apart(dve, r_dve, done + 3, passed)
                        nc.vector.match_replace(picked[:], top8[:], lg[:], 0.0).then_inc(r_dve, 1)
                        after(dve, r_dve, done + 4)
                        nc.vector.tensor_tensor(picked[:], lg[:], picked[:], ALU.subtract).then_inc(r_dve, 1)
            run_batches(dve, step)

        @block.tensor
        def _(pe):
            mm, turn = nc.tensor.matmul, nc.tensor.transpose
            HALVES = ((0, 0), (0, 1), (1, 0))

            def turn_tiles(src, i, done):
                for c in range(2):
                    for t in range(TT):
                        last = turn(M[:, T * c + P * t:T * c + P * t + P], src[:, t, P * (2 * i + c):P * (2 * i + c) + P],
                                    ident[:])
                last.then_inc(done, 1)

            def project_T(w, act_T, i, c, done):
                for n, (hw, ha) in enumerate(HALVES):
                    for k in range(KC):
                        last = mm(A[i][:, T * c:T * c + T], w[:, hw, k, P * (2 * i + c):P * (2 * i + c) + P],
                                  act_T[:, ha, k, :], start=(n == 0 and k == 0), stop=(n == 2 and k == KC - 1))
                if c == 1:
                    last.then_inc(done, 1)

            def project(w, act_T, i, half, done):
                for k in (2 * half, 2 * half + 1):
                    for n, (ha, hw) in enumerate(HALVES):
                        last = mm(A[i][:, :], act_T[:, ha, k, P * i:P * i + P], w[:, hw, k, :],
                                  start=(k == 0 and n == 0), stop=(k == KC - 1 and n == 2))
                if half == 1:
                    last.then_inc(done, 1)

            def spread(b, jp):
                after(pe, rden_out, 2 * b + jp + 1)
                for j in range(2):
                    for q in range(TT):
                        last = turn(M[:, T * j + P * q:T * j + P * q + P],
                                    rden[:, q, 4 * j:4 * j + 4, :].rearrange("p h d -> p (h d)"), ident[:])
                last.then_inc(rden_mm, 1)

            def most(count, bound):
                return min(count, bound) if isinstance(count, int) else count

            def step(b, g, k):
                attn, prep, fin, ahead = has(b, 0, B), has(b, -1, B - 1), has(b, 1, B + 1), has(b, -2, B - 2)
                routing = has(b, GB + 1, B + 2) and k == 1
                end = isinstance(b, int)
                q = (k - 1) % GB
                for s in range(H):
                    if attn:
                        if s % 4 == 0:
                            after(pe, q_in[s // 4], 64 * (b + 1))
                            after(pe, k_in[s // 4], 64 * (b + 1))
                        after(pe, expd, H * b + s - 1)
                        for qt in range(TT):
                            last = mm(S[s % 2][:, T * qt:T * qt + T], q_stack[:, s, P * qt:P * qt + P], k_stack[:, s, :],
                                      start=True, stop=True)
                        last.then_inc(score, 1)
                    if attn if s >= 2 else fin:
                        bb, hh = (b if s >= 2 else b - 1), (s - 2) % H
                        after(pe, expd, H * bb + hh + 1)
                        after(pe, pT_dve if hh % 2 else pT_act, 8 * bb + hh // 2)
                        for kt in range(TT):
                            for qt in range(TT):
                                last = turn(TP[hh % 2][:, T * kt + P * qt:T * kt + P * qt + P],
                                            pr[:, hh % 2, qt, P * kt:P * kt + P], ident[:])
                        last.then_inc(turned, 1)
                    if s % 4 == 2 and (attn if s >= 6 else fin):
                        bb, j = (b, s // 4 - 1) if s >= 6 else (b - 1, 3)
                        after(pe, pT_act, 8 * bb + 2 * j + 2)
                        after(pe, pT_dve, 8 * bb + 2 * j + 2)
                        after(pe, v_out, 2 * (bb + 1))
                        after(pe, o_norm, 2 * bb + j // 2)
                        vp = (k if s >= 6 else k - 1) % 2
                        for kt in range(TT):
                            for c in range(4):
                                last = mm(O[32 * c:32 * c + 32, T * (j % 2):T * (j % 2) + T],
                                          v[:, vp, kt, DK * (4 * j + c):DK * (4 * j + c) + DK], pT[:, c, kt, :],
                                          start=(kt == 0), stop=(kt == TT - 1), skip_group_check=True)
                        last.then_inc(pv, 1)

                    if s == 1 and fin:
                        after(pe, lg_out, b - 1)
                        if end:
                            after(pe, xT_lo, most(2 * (b + 2), 2 * B))
                        spread(b - 1, 1)
                    if s == 2 and prep:
                        after(pe, c_in, 16 * (b + 2))
                        after(pe, o_scale, 2 * b)
                        if end:
                            after(pe, xT_lo, most(2 * (b + 2), 2 * B))
                        turn_tiles(ct, 0, cT_mm)
                    if s == 3 and routing:
                        after(pe, cT_lo, most(2 * (b + 1) + 1, 2 * B))
                        if end:
                            after(pe, lg_out, b - 1)
                            after(pe, o_scale, most(2 * b, 2 * B))
                        after(pe, r_dve, N_RDVE * g)
                        for t in range(TT):
                            last = turn(M[:, P * t:P * t + P], picked[:, P * t:P * t + P], ident[:])
                        last.then_inc(r_t, 1)
                    if s == 4 and routing:
                        after(pe, r_tout, g)
                        for t in range(TT):
                            for kk in range(GB):
                                last = mm(M[E * kk:E * kk + E, :], pickedT[:, t, E * kk:E * kk + E], x2[:, kk, t, :],
                                          start=(t == 0), stop=(t == TT - 1), skip_group_check=True)
                        last.then_inc(r_m, 1)
                    if s == 5 and routing:
                        after(pe, r_mout, g)
                        for c in range(KC):
                            last = turn(M[:, P * c:P * c + P], merged[:, P * c:P * c + P], ident[:])
                        last.then_inc(r_mt, 1)
                    if s == 6 and prep:
                        after(pe, cT_lo, 2 * (b + 1) + 1)
                        if k == 1:
                            after(pe, r_mtout, g)
                        turn_tiles(ct, 1, cT_mm)
                    if s == 9 and attn:
                        after(pe, cT_lo, most(2 * (b + 2), 2 * B))
                        if end:
                            after(pe, o_scale, 2 * b)
                        spread(b, 0)
                    if s == 10 and ahead:
                        after(pe, n1_out, 2 * (b + 3))
                        after(pe, o_scale, 2 * b + 1)
                        if end:
                            after(pe, cT_lo, 2 * (b + 2))
                        turn_tiles(xt, 0, xT_mm)
                    if s == 12 and ahead:
                        after(pe, xT_lo, 2 * (b + 2) + 1)
                        turn_tiles(xt, 1, xT_mm)
                    if s == 14 and fin:
                        after(pe, x2T_out, 2 * (b - 1) + 1)
                        turn_tiles(x2[:, q, :, :], 1, x2T_mm)
                    if s == 15 and fin:
                        after(pe, x2T_out, 2 * b)
                        for c in range(KC):
                            last = mm(M[E * q:E * q + E, 0:T], gwT[:, c, :], x2T[:, c, :], start=(c == 0),
                                      stop=(c == KC - 1))
                        last.then_inc(lg_mm, 1)

                    i, half = s // 2 % 2, s % 2
                    if s < 4 and prep:
                        if half == 0:
                            after(pe, v_out, 2 * b + i + 1)
                            after(pe, xT_lo, 2 * (b + 2))
                        project_T(w_q, xT, i, half, q_mm)
                    if 4 <= s < 8 and fin:
                        if half == 0:
                            if prep:
                                after(pe, q_lo, 2 * (b + 1) + i + 1)
                            else:
                                after(pe, v_out, 2 * B)
                                after(pe, x2_sum, 2 * (b - 1))
                        after(pe, o_lo, 2 * (b - 1) + half + 1)
                        project(w_o, oT, i, half, o_mm)
                    if 8 <= s < 12 and prep:
                        if half == 0:
                            after(pe, x2_sum, 2 * (b - 1) + i + 1)
                            if end:
                                after(pe, q_lo, 2 * (b + 1) + i + 1)
                            after(pe, cT_lo, 2 * (b + 2))
                        project_T(w_k, cT, i, half, k_mm)
                    if s >= 12 and prep:
                        if half == 0:
                            after(pe, k_lo, 2 * (b + 1) + i + 1)
                        project(w_v, cT, i, half, v_mm)

                    if s == 13 and fin:
                        after(pe, n2_out, 2 * b)
                        after(pe, xT_lo, most(2 * (b + 3), 2 * B))
                        if end:
                            after(pe, o_scale, most(2 * b + 1, 2 * B))
                        turn_tiles(x2[:, q, :, :], 0, x2T_mm)
            run_batches(pe, step)


def experts(nc, sh, jt, w1, w2, g_ffn, out, picked_dram, outs_dram):
    st = ExitStack()
    with st:
        sb = lambda name, shape, dt=F32: st.enter_context(nc.sbuf_tensor(name, shape, dt))
        ps = lambda name: st.enter_context(nc.psum_tensor(name, [P, 512], F32))
        sem = lambda name: st.enter_context(nc.semaphore(name))
        ring, m_raw, ident, fold, ones, piece_in = sh.ring, sh.m_raw, sh.ident, sh.fold, sh.ones, sh.piece_in
        m = sb("m", [P, 2, KC, B])
        w1b, w2b, bias_in = sh.w1b, sh.w2b, sh.bias_in
        h = sb("h", [P, 2, D])
        hT = sb("hT", [P, 2, KC, P])
        part = sb("part", [P, 2, D])
        o = sb("o", [B, 2, D])
        HP = [ps("HP0"), ps("HP1")]
        TPh = [ps("TPh0"), ps("TPh1")]
        OP = [ps("OP0"), ps("OP1")]
        FP = [ps("FP0"), ps("FP1")]
        m_out, h_mm, h_out, t_mm, t_out, o_mm, o_out, f_mm, f_out = (
            sem(n) for n in ("fm_out", "h_mm", "h_out", "t_mm", "t_out", "fo_mm", "fo_out", "f_mm", "f_out"))
        stored = [sem("stored0"), sem("stored1")]
        block = st.enter_context(nc.Block())
        NP = E // 2

        @block.sync
        def _(sp):
            def expert(e, n):
                for i in range(PER):
                    after(sp, h_mm if i < KC else o_mm, e - 1)
                    sh.load_piece(sp, w1, w2, e, n, i)
            for i in range(EARLY, SLOTS):
                sh.load_piece(sp, w1, w2, 1, 1, i - PER)
            with sp.Fori(1, NP) as i:
                expert(i * 2, 0)
                expert(i * 2 + 1, 1)
            sp.dma_start(jt.gate[:, 0:1], g_ffn.rearrange("(a n) -> a n", a=1).broadcast_to([P, 1])).then_inc(jt.g_in, 16)
            for n in range(2):
                sp.wait_ge(stored[n], 16 * (NP - 1))
            for k in range(GB):
                sp.dma_start(jt.outs[E * k:E * k + E - 2, :, :],
                             outs_dram[0:E - 2, NG * k:NG * k + NG, :]).then_inc(jt.outs_in, 16)
            sp.wait_ge(o_mm, E - 1)
            for n in range(2 * GB):
                jt.load_x(sp, out, 0, n)
            sp.wait_ge(jt.zeroed, 1)
            for n in range(2 * GB):
                jt.load_picked(sp, picked_dram, 0, n)
            for n in range(2):
                sp.wait_ge(f_out, E - 1 + n)
                for k in range(GB):
                    sp.dma_start(jt.outs[E * k + E - 2 + n:E * k + E - 1 + n, :, :],
                                 o[NG * k:NG * k + NG, n, :]).then_inc(jt.outs_in, 16)

        @block.gpsimd
        def _(pool):
            def biases(e, n):
                after(pool, o_mm, e - 1)
                sh.load_biases(pool, w1, w2, e, n)

            def store(e, n):
                after(pool, f_out, e + 1)
                pool.dma_start(outs_dram[e], o[:, n, :]).then_inc(stored[n], 16)
            with pool.Fori(1, NP) as i:
                for n in range(2):
                    store(i * 2 + n - 2, n)
                    biases(i * 2 + n, n)
            pool.wait_ge(o_mm, E - 1)
            pool.memset(jt.pz[:], 0.0).then_inc(jt.zeroed, 1)

        @block.scalar
        def _(act):
            def expert(e, n, i):
                after(act, h_mm, e + 1)
                after(act, t_mm, e - 1)
                nc.scalar.activation(h[:, n, :], HP[n][:, :], ACT.Gelu).then_inc(h_out, 1)
                after(act, f_mm, e + 1)
                after(act, stored[n], i * 16)
                nc.scalar.activation(o[:, n, :], FP[n][0:B, :], ACT.Copy).then_inc(f_out, 1)
            expert(0, 0, 0)
            expert(1, 1, 0)
            with act.Fori(1, NP) as i:
                expert(i * 2, 0, i)
                expert(i * 2 + 1, 1, i)

        @block.vector
        def _(dve):
            dve.wait_ge(sh.m_in, 16)

            def expert(e, n):
                after(dve, h_mm, e - 1)
                nc.vector.tensor_copy(m[:, n, :, :].rearrange("p c (k g) -> p c k g", k=GB),
                                      m_raw[:, :, :, :, e].rearrange("p g c k -> p c k g")).then_inc(m_out, 1)
                after(dve, t_mm, e + 1)
                after(dve, o_mm, e - 1)
                nc.vector.tensor_copy(hT[:, n, :, :].rearrange("p s m -> p (s m)"), TPh[n][:, :]).then_inc(t_out, 1)
                after(dve, o_mm, e + 1)
                after(dve, f_mm, e - 1)
                nc.vector.tensor_copy(part[:, n, :], OP[n][:, :]).then_inc(o_out, 1)
            expert(0, 0)
            expert(1, 1)
            with dve.Fori(1, NP) as i:
                expert(i * 2, 0)
                expert(i * 2 + 1, 1)

        @block.tensor
        def _(pe):
            mm, turn = nc.tensor.matmul, nc.tensor.transpose
            def expert(e, n, i):
                after(pe, m_out, e + 1)
                after(pe, h_out, e - 1)
                after(pe, bias_in[n], 32 * i + 32)
                for k in range(KC):
                    after(pe, piece_in[PER * n + k], 16 * i + 16)
                    for c in range(HC):
                        last = mm(HP[n][B * c:B * c + B, :], m[:, n, k, :], ring[:, PER * n + k, D * c:D * c + D],
                                  start=(k == 0), stop=False, skip_group_check=True)
                for c in range(HC):
                    last = mm(HP[n][B * c:B * c + B, :], ones[:, 0:B], w1b[:, n, D * c:D * c + D], start=False, stop=True,
                              skip_group_check=True)
                last.then_inc(h_mm, 1)
                after(pe, h_out, e + 1)
                after(pe, t_out, e - 1)
                for s in range(KC):
                    last = turn(TPh[n][:, P * s:P * s + P], h[:, n, s:D:KC], ident[:])
                last.then_inc(t_mm, 1)
                after(pe, t_out, e + 1)
                after(pe, o_out, e - 1)
                for c in range(HC):
                    after(pe, piece_in[PER * n + KC + c], 16 * i + 16)
                for s in range(KC):
                    for c in range(HC):
                        last = mm(OP[n][B * c:B * c + B, :], hT[:, n, s, B * c:B * c + B],
                                  ring[:, PER * n + KC + c, D * s:D * s + D], start=(s == 0), stop=(s == KC - 1 and c > 0),
                                  skip_group_check=True)
                last = mm(OP[n][0:B, :], ones[:, 0:B], w2b[:, n, :], start=False, stop=True, skip_group_check=True)
                last.then_inc(o_mm, 1)
                after(pe, o_out, e + 1)
                after(pe, f_out, e - 1)
                mm(FP[n][0:B, :], fold[:], part[:, n, :], start=True, stop=True).then_inc(f_mm, 1)

            expert(0, 0, 0)
            expert(1, 1, 0)
            with pe.Fori(1, NP) as i:
                expert(i * 2, 0, i)
                expert(i * 2 + 1, 1, i)


def combine(nc, jt, out, picked_dram):
    st = ExitStack()
    with st:
        sem = lambda name: st.enter_context(nc.semaphore(name))
        xr, pz, gate, x_in, p_in = jt.xr, jt.pz, jt.gate, jt.x_in, jt.p_in
        Y = [st.enter_context(nc.psum_tensor(f"Y{i}", [P, D], F32)) for i in range(8)]
        N = 2 * GB
        x_out = [sem(f"x_out_f{i}") for i in range(N)]
        gated, y_mm, y_sum = (sem(n) for n in ("gated", "y_mm", "y_sum"))
        block = st.enter_context(nc.Block())

        def turns(eng, turn):
            turn(0)
            with eng.Fori(1, B // N) as i:
                turn(i)

        @block.sync
        def _(sp):
            with sp.Fori(1, B // N) as i:
                for n in range(N):
                    after(sp, y_mm, i * 2 * N + 2 * (n + 1) - 2 * N)
                    jt.load_picked(sp, picked_dram, i, n)
                    after(sp, x_out[n], i * 16)
                    jt.load_x(sp, out, i, n)

        @block.scalar
        def _(act):
            act.wait_ge(jt.g_in, 16)
            act.activation(gate[:, 1:2], gate[:, 0:1], ACT.Tanh).then_inc(gated, 1)

            def turn(i):
                for n in range(N):
                    after(act, y_sum, i * 2 * N + 2 * (n + 1))
                    act.dma_start(out[i * N + n].rearrange("(t p) n -> p t n", p=P), xr[:, n // GB, n % GB, :, :]).then_inc(x_out[n], 16)
            turns(act, turn)
            for n in range(N):
                act.wait_ge(x_out[n], 16 * (B // N))

        @block.vector
        def _(dve):
            dve.wait_ge(gated, 1)

            def turn(i):
                for n in range(N):
                    after(dve, x_in[n], i * 16 + 16)
                    for t in range(TT):
                        after(dve, y_mm, i * 2 * N + 2 * n + t + 1)
                        x_t = xr[:, n // GB, n % GB, t, :]
                        nc.vector.scalar_tensor_tensor(x_t, Y[(2 * n + t) % 8][:, :], gate[:, 1:2], x_t, ALU.mult,
                                                       ALU.add).then_inc(y_sum, 1)
            turns(dve, turn)

        @block.tensor
        def _(pe):
            pe.wait_ge(jt.outs_in, 16 * 3 * GB)

            def turn(i):
                for n in range(N):
                    after(pe, p_in[n], i * 16 + 16)
                    for t in range(TT):
                        after(pe, y_sum, i * 2 * N + 2 * n + t + 1 - 8)
                        nc.tensor.matmul(Y[(2 * n + t) % 8][:, :], pz[:, n // GB, n % GB, P * t:P * t + P],
                                         jt.outs[:, i * 2 + n // GB, :], start=True, stop=True).then_inc(y_mm, 1)
            turns(pe, turn)


def build(nc, A, out):
    merged_dram = nc.dram_tensor("merged_scratch", [NG - 1, P, KC, P], F32, kind="Internal").ap()
    picked_dram = nc.dram_tensor("picked_scratch", [NG, P, T], F32, kind="Internal").ap()
    outs_dram = nc.dram_tensor("outs_scratch", [E - 2, B, D], F32, kind="Internal").ap()
    with ExitStack() as st:
        sh = Shared(nc, st)
        attention_and_routing(nc, sh, A["L0_ffn_w1"], A["L0_ffn_w2"], A["x"], A["ctx_1024"], A["g_xattn"], A["L0_xattn_Wq"], A["L0_xattn_bq"], A["L0_xattn_Wk"],
                              A["L0_xattn_bk"], A["L0_xattn_Wv"], A["L0_xattn_bv"], A["L0_xattn_Wo"], A["L0_xattn_bo"],
                              A["L0_ffn_gate_w"], A["L0_ffn_gate_b"], out, merged_dram, picked_dram)
        jt = Joint(nc, st, sh)
        experts(nc, sh, jt, A["L0_ffn_w1"], A["L0_ffn_w2"], A["g_ffn"], out, picked_dram, outs_dram)
        combine(nc, jt, out, picked_dram)


def kernel(**inputs):
    import concourse.bacc as bacc
    from concourse.bass_utils import run_bass_kernel_spmd

    nc = bacc.Bacc("TRN2", target_bir_lowering=False, num_devices=1)
    arrays, aps = {}, {}
    for name, a in inputs.items():
        a = np.ascontiguousarray(a)
        arrays[name + "_in"] = a
        aps[name] = nc.dram_tensor(name + "_in", a.shape, mybir.dt.from_np(a.dtype), kind="ExternalInput").ap()
    out = nc.dram_tensor("y_out", [B, T, D], F32, kind="ExternalOutput").ap()
    build(nc, aps, out)
    return run_bass_kernel_spmd(nc, [arrays], core_ids=[0]).results[0]["y_out"]
```
